# Optimizing a Trainium2 kernel written in Bass

```python
import numpy as np
import jax
import jax.numpy as jnp

def _softmax(x, axis=-1):
    return jax.nn.softmax(x, axis=axis)

def _gelu(x):
    return jax.nn.gelu(x, approximate=True)

def _silu(x):
    return jax.nn.silu(x)

def _sigmoid(x):
    return jax.nn.sigmoid(x)

def _layernorm(x, axis=-1, eps=1e-05):
    m = jnp.mean(x, axis=axis, keepdims=True)
    v = jnp.var(x, axis=axis, keepdims=True)
    return (x - m) / jnp.sqrt(v + eps)

def _scatter_add(tgt, idx, src, axis=0):
    return tgt.at[idx].add(src)

def _segment_sum(src, seg, n):
    return jax.ops.segment_sum(src, seg, n)
kernel_name = 'mk_dlrm_tower_d1_rec_r8_39e909'

def setup_inputs(seed: int=0):
    np.random.seed(seed)
    _w = jnp.asarray

    def _rec_inputs():
        import jax
        import jax.numpy as jnp
        _tk = jax.random.key(seed)
        ids = jnp.stack([jax.random.randint(jax.random.fold_in(_tk, 200 + f), (1024,), 0, v, jnp.int32) for f, v in enumerate([125000, 1250, 1000, 1250, 12500, 1250, 12500, 12500, 1250, 1250, 1250, 12500, 12500, 12500, 1250, 12500, 12500, 1000, 1250, 1250, 1250, 1000, 1000, 1000, 1250, 1250, 1000, 1000, 1250, 1000, 1250, 1000, 1000])], axis=1)
        tbl_0 = 0.05 * jax.random.normal(jax.random.fold_in(_tk, 500 + 0), (125000, 128), jnp.float32)
        tbl_1 = 0.05 * jax.random.normal(jax.random.fold_in(_tk, 500 + 1), (1250, 128), jnp.float32)
        tbl_2 = 0.05 * jax.random.normal(jax.random.fold_in(_tk, 500 + 2), (1000, 128), jnp.float32)
        tbl_3 = 0.05 * jax.random.normal(jax.random.fold_in(_tk, 500 + 3), (1250, 128), jnp.float32)
        tbl_4 = 0.05 * jax.random.normal(jax.random.fold_in(_tk, 500 + 4), (12500, 128), jnp.float32)
        tbl_5 = 0.05 * jax.random.normal(jax.random.fold_in(_tk, 500 + 5), (1250, 128), jnp.float32)
        tbl_6 = 0.05 * jax.random.normal(jax.random.fold_in(_tk, 500 + 6), (12500, 128), jnp.float32)
        tbl_7 = 0.05 * jax.random.normal(jax.random.fold_in(_tk, 500 + 7), (12500, 128), jnp.float32)
        tbl_8 = 0.05 * jax.random.normal(jax.random.fold_in(_tk, 500 + 8), (1250, 128), jnp.float32)
        tbl_9 = 0.05 * jax.random.normal(jax.random.fold_in(_tk, 500 + 9), (1250, 128), jnp.float32)
        tbl_10 = 0.05 * jax.random.normal(jax.random.fold_in(_tk, 500 + 10), (1250, 128), jnp.float32)
        tbl_11 = 0.05 * jax.random.normal(jax.random.fold_in(_tk, 500 + 11), (12500, 128), jnp.float32)
        tbl_12 = 0.05 * jax.random.normal(jax.random.fold_in(_tk, 500 + 12), (12500, 128), jnp.float32)
        tbl_13 = 0.05 * jax.random.normal(jax.random.fold_in(_tk, 500 + 13), (12500, 128), jnp.float32)
        tbl_14 = 0.05 * jax.random.normal(jax.random.fold_in(_tk, 500 + 14), (1250, 128), jnp.float32)
        tbl_15 = 0.05 * jax.random.normal(jax.random.fold_in(_tk, 500 + 15), (12500, 128), jnp.float32)
        tbl_16 = 0.05 * jax.random.normal(jax.random.fold_in(_tk, 500 + 16), (12500, 128), jnp.float32)
        tbl_17 = 0.05 * jax.random.normal(jax.random.fold_in(_tk, 500 + 17), (1000, 128), jnp.float32)
        tbl_18 = 0.05 * jax.random.normal(jax.random.fold_in(_tk, 500 + 18), (1250, 128), jnp.float32)
        tbl_19 = 0.05 * jax.random.normal(jax.random.fold_in(_tk, 500 + 19), (1250, 128), jnp.float32)
        tbl_20 = 0.05 * jax.random.normal(jax.random.fold_in(_tk, 500 + 20), (1250, 128), jnp.float32)
        tbl_21 = 0.05 * jax.random.normal(jax.random.fold_in(_tk, 500 + 21), (1000, 128), jnp.float32)
        tbl_22 = 0.05 * jax.random.normal(jax.random.fold_in(_tk, 500 + 22), (1000, 128), jnp.float32)
        tbl_23 = 0.05 * jax.random.normal(jax.random.fold_in(_tk, 500 + 23), (1000, 128), jnp.float32)
        tbl_24 = 0.05 * jax.random.normal(jax.random.fold_in(_tk, 500 + 24), (1250, 128), jnp.float32)
        tbl_25 = 0.05 * jax.random.normal(jax.random.fold_in(_tk, 500 + 25), (1250, 128), jnp.float32)
        tbl_26 = 0.05 * jax.random.normal(jax.random.fold_in(_tk, 500 + 26), (1000, 128), jnp.float32)
        tbl_27 = 0.05 * jax.random.normal(jax.random.fold_in(_tk, 500 + 27), (1000, 128), jnp.float32)
        tbl_28 = 0.05 * jax.random.normal(jax.random.fold_in(_tk, 500 + 28), (1250, 128), jnp.float32)
        tbl_29 = 0.05 * jax.random.normal(jax.random.fold_in(_tk, 500 + 29), (1000, 128), jnp.float32)
        tbl_30 = 0.05 * jax.random.normal(jax.random.fold_in(_tk, 500 + 30), (1250, 128), jnp.float32)
        tbl_31 = 0.05 * jax.random.normal(jax.random.fold_in(_tk, 500 + 31), (1000, 128), jnp.float32)
        tbl_32 = 0.05 * jax.random.normal(jax.random.fold_in(_tk, 500 + 32), (1000, 128), jnp.float32)
        _rk = jax.random.fold_in(_tk, 7)
        r_gnn_feature = -0.00340659 + 1.00146 * jax.random.normal(jax.random.fold_in(_rk, 101), (1024, 128), jnp.float32)
        W_top1 = 0.051031 * jax.random.normal(jax.random.fold_in(_tk, 801), (384, 512), jnp.float32)
        W_top2 = 0.0441942 * jax.random.normal(jax.random.fold_in(_tk, 802), (512, 256), jnp.float32)
        W_top3 = 0.0625 * jax.random.normal(jax.random.fold_in(_tk, 803), (256, 1), jnp.float32)
        b_top1 = jnp.zeros((512,), jnp.float32)
        b_top2 = jnp.zeros((256,), jnp.float32)
        return (r_gnn_feature, ids, tbl_0, tbl_1, tbl_2, tbl_3, tbl_4, tbl_5, tbl_6, tbl_7, tbl_8, tbl_9, tbl_10, tbl_11, tbl_12, tbl_13, tbl_14, tbl_15, tbl_16, tbl_17, tbl_18, tbl_19, tbl_20, tbl_21, tbl_22, tbl_23, tbl_24, tbl_25, tbl_26, tbl_27, tbl_28, tbl_29, tbl_30, tbl_31, tbl_32, W_top1, b_top1, W_top2, b_top2, W_top3)
    r_gnn_feature, ids, tbl_0, tbl_1, tbl_2, tbl_3, tbl_4, tbl_5, tbl_6, tbl_7, tbl_8, tbl_9, tbl_10, tbl_11, tbl_12, tbl_13, tbl_14, tbl_15, tbl_16, tbl_17, tbl_18, tbl_19, tbl_20, tbl_21, tbl_22, tbl_23, tbl_24, tbl_25, tbl_26, tbl_27, tbl_28, tbl_29, tbl_30, tbl_31, tbl_32, W_top1, b_top1, W_top2, b_top2, W_top3 = _rec_inputs()

    def _L0_rec_setup():
        import jax, jax.numpy as jnp
        import numpy as np
        B, F, D, A = (1024, 33, 128, 128)
        key = jax.random.key(seed)
        k1, k2, k3, k4 = jax.random.split(key, 4)
        gnn_feature = jax.random.normal(k1, (B, A), dtype=jnp.float32)
        x = jax.random.normal(k2, (B, F, D), dtype=jnp.float32)
        lim = 1.0 / np.sqrt(D)
        attn_W = jax.random.uniform(k3, (A, D), minval=-lim, maxval=lim, dtype=jnp.float32)
        attn_b = jax.random.uniform(k4, (A,), minval=-lim, maxval=lim, dtype=jnp.float32)
        return {'gnn_feature': gnn_feature, 'x': x, 'attn_W': attn_W, 'attn_b': attn_b}
    _L0_rec_all = _L0_rec_setup()
    _L0_rec_in = {k: v for k, v in _L0_rec_all.items() if k in ('attn_W', 'attn_b')}
    del _L0_rec_all
    return {'r_gnn_feature': r_gnn_feature, 'ids': ids, 'tbl_0': tbl_0, 'tbl_1': tbl_1, 'tbl_2': tbl_2, 'tbl_3': tbl_3, 'tbl_4': tbl_4, 'tbl_5': tbl_5, 'tbl_6': tbl_6, 'tbl_7': tbl_7, 'tbl_8': tbl_8, 'tbl_9': tbl_9, 'tbl_10': tbl_10, 'tbl_11': tbl_11, 'tbl_12': tbl_12, 'tbl_13': tbl_13, 'tbl_14': tbl_14, 'tbl_15': tbl_15, 'tbl_16': tbl_16, 'tbl_17': tbl_17, 'tbl_18': tbl_18, 'tbl_19': tbl_19, 'tbl_20': tbl_20, 'tbl_21': tbl_21, 'tbl_22': tbl_22, 'tbl_23': tbl_23, 'tbl_24': tbl_24, 'tbl_25': tbl_25, 'tbl_26': tbl_26, 'tbl_27': tbl_27, 'tbl_28': tbl_28, 'tbl_29': tbl_29, 'tbl_30': tbl_30, 'tbl_31': tbl_31, 'tbl_32': tbl_32, 'W_top1': W_top1, 'b_top1': b_top1, 'W_top2': W_top2, 'b_top2': b_top2, 'W_top3': W_top3, 'L0_rec_attn_W': _L0_rec_in['attn_W'], 'L0_rec_attn_b': _L0_rec_in['attn_b']}

def reference(r_gnn_feature, ids, tbl_0, tbl_1, tbl_2, tbl_3, tbl_4, tbl_5, tbl_6, tbl_7, tbl_8, tbl_9, tbl_10, tbl_11, tbl_12, tbl_13, tbl_14, tbl_15, tbl_16, tbl_17, tbl_18, tbl_19, tbl_20, tbl_21, tbl_22, tbl_23, tbl_24, tbl_25, tbl_26, tbl_27, tbl_28, tbl_29, tbl_30, tbl_31, tbl_32, W_top1, b_top1, W_top2, b_top2, W_top3, L0_rec_attn_W, L0_rec_attn_b):
    import jax
    import jax.numpy as jnp

    def _L0_rec_ref(gnn_feature, x, attn_W, attn_b):
        import jax, jax.numpy as jnp
        import numpy as np
        B, F, D, A = (1024, 33, 128, 128)
        num_fields = x.shape[1]
        row, col = np.triu_indices(num_fields, k=1)
        inner = x[:, row] * x[:, col]
        fm = jax.nn.relu(jnp.einsum('bpd,ad->bpa', inner, attn_W) + attn_b)
        scores = jnp.einsum('ba,bpa->bp', gnn_feature, fm)
        attn = jax.nn.softmax(scores, axis=1)
        attn_output = jnp.einsum('bp,bpd->bd', attn, inner) * 100.0
        return jnp.concatenate([gnn_feature, attn_output], axis=1)
    e = jnp.stack([tbl_0[ids[:, 0]], tbl_1[ids[:, 1]], tbl_2[ids[:, 2]], tbl_3[ids[:, 3]], tbl_4[ids[:, 4]], tbl_5[ids[:, 5]], tbl_6[ids[:, 6]], tbl_7[ids[:, 7]], tbl_8[ids[:, 8]], tbl_9[ids[:, 9]], tbl_10[ids[:, 10]], tbl_11[ids[:, 11]], tbl_12[ids[:, 12]], tbl_13[ids[:, 13]], tbl_14[ids[:, 14]], tbl_15[ids[:, 15]], tbl_16[ids[:, 16]], tbl_17[ids[:, 17]], tbl_18[ids[:, 18]], tbl_19[ids[:, 19]], tbl_20[ids[:, 20]], tbl_21[ids[:, 21]], tbl_22[ids[:, 22]], tbl_23[ids[:, 23]], tbl_24[ids[:, 24]], tbl_25[ids[:, 25]], tbl_26[ids[:, 26]], tbl_27[ids[:, 27]], tbl_28[ids[:, 28]], tbl_29[ids[:, 29]], tbl_30[ids[:, 30]], tbl_31[ids[:, 31]], tbl_32[ids[:, 32]]], axis=1)
    z = _L0_rec_ref(r_gnn_feature, e, L0_rec_attn_W, L0_rec_attn_b)
    z = z.reshape(z.shape[0], -1)
    h = jnp.concatenate([z, r_gnn_feature], axis=1)
    h = jnp.maximum(h @ W_top1 + b_top1, 0.0)
    h = jnp.maximum(h @ W_top2 + b_top2, 0.0)
    y = h @ W_top3
    return y

_drawn_inputs = setup_inputs


def setup_inputs(seed=0):
    import zlib

    import numpy as np

    out = dict(_drawn_inputs(seed))
    spreads = {'b_top1': (0.0, 0.464), 'b_top2': (0.0, 0.1)}
    factors = {'tbl_0': 8.0,
     'tbl_1': 8.0,
     'tbl_2': 8.0,
     'tbl_3': 8.0,
     'tbl_4': 8.0,
     'tbl_5': 8.0,
     'tbl_6': 8.0,
     'tbl_7': 8.0,
     'tbl_8': 8.0,
     'tbl_9': 8.0,
     'tbl_10': 8.0,
     'tbl_11': 8.0,
     'tbl_12': 8.0,
     'tbl_13': 8.0,
     'tbl_14': 8.0,
     'tbl_15': 8.0,
     'tbl_16': 8.0,
     'tbl_17': 8.0,
     'tbl_18': 8.0,
     'tbl_19': 8.0,
     'tbl_20': 8.0,
     'tbl_21': 8.0,
     'tbl_22': 8.0,
     'tbl_23': 8.0,
     'tbl_24': 8.0,
     'tbl_25': 8.0,
     'tbl_26': 8.0,
     'tbl_27': 8.0,
     'tbl_28': 8.0,
     'tbl_29': 8.0,
     'tbl_30': 8.0,
     'tbl_31': 8.0,
     'tbl_32': 8.0,
     'L0_rec_attn_W': 8.0,
     'L0_rec_attn_b': 8.0}
    for name, (base, spread) in spreads.items():
        noise = np.random.default_rng([zlib.crc32(name.encode()), seed]).standard_normal(out[name].shape)
        drawn = base * np.exp(spread * noise) if base else spread * noise
        out[name] = jnp.asarray(drawn.astype(out[name].dtype))
    for name, factor in factors.items():
        out[name] = (out[name] * factor).astype(out[name].dtype)
    return out
```

```python
import concourse.bass as bass
from concourse import mybir
from contextlib import ExitStack

FP32 = mybir.dt.float32
BF16 = mybir.dt.bfloat16
I32 = mybir.dt.int32
ALU = mybir.AluOpType
ACT = mybir.ActivationFunctionType
AX = mybir.AxisListType


class Tile:

    def __init__(self, loop, ahead):
        self.loop, self.ahead = loop, ahead

    def __add__(self, n):
        return Tile(self.loop, self.ahead + n)

    def __sub__(self, n):
        return Tile(self.loop, self.ahead - n)

    def times(self, each, more=0):
        if isinstance(self.loop, int):
            return (self.loop + self.ahead) * each + more
        return self.loop * each + (self.ahead * each + more)

    def odd(self):
        return (self.loop + self.ahead) % 2

    def below(self, n):
        return isinstance(self.loop, int) and self.loop + self.ahead < n


def afm_tower(nc, gnn, ids, tables, w1, b1, w2, b2, w3, attn_w, attn_b, out):
    P = 128
    B, D = gnn.shape
    F = len(tables)
    T = B // P
    K = (F - 1) // 2
    FX = F + K
    PAIRS = K * F
    HALF = PAIRS // 2
    GROUPS = 4
    STEPS = P // GROUPS
    H1, H2 = w1.shape[1], w2.shape[1]
    K1, M1, K2, M2 = w1.shape[0] // P, H1 // P, H2 and H1 // P, H2 // P
    FB = 4
    FCH = -(-F // FB)
    YS = 8
    YR = P // YS
    ODD = range(2)

    jobs = {s: [] for s in range(STEPS)}
    for c in range(FCH):
        jobs[2 + c // 2].append(("attn_t", c))
        jobs[STEPS - 3 - FCH + c].append(("x_t", c))
    for r in range(YR):
        jobs[7 + r // 2].append(("fields", r))
    for n in range(3):
        jobs[15 + n + (n > 0)].append(("mlp", n))
    bank_of, n = {}, 0
    for s in range(STEPS):
        for job in jobs[s]:
            bank_of[job] = n % 2
            n += 1

    ctx = ExitStack()
    with ctx:
        def sb(name, shape, dt=FP32):
            return ctx.enter_context(nc.sbuf_tensor(name, shape, dt))

        def pb(name, shape):
            return ctx.enter_context(nc.psum_tensor(name, shape, FP32))

        def sem(name):
            return ctx.enter_context(nc.semaphore(name))

        ids_all = sb("ids_all", [P, T, F], I32)
        ids_now = sb("ids_now", [P, F], I32)
        ids_seen = sb("ids_seen", [P, 1], I32)
        x_rows = sb("x_rows", [P, F, D])
        xt = sb("xt", [D, 2, P, FX])
        inner = sb("inner", [D, 2, GROUPS * PAIRS])
        fm = sb("fm", [P, 2, GROUPS * PAIRS])
        gnn_blocks = sb("gnn_blocks", [P, GROUPS, STEPS, STEPS])
        x_fields = sb("x_fields", [P, P // 2, D])
        attn_rows = sb("attn_rows", [P, F * 2 * FX])
        exp_rows = sb("exp_rows", [P, PAIRS])
        attn_t = sb("attn_t", [2 * FX, F, P])
        weighted = sb("weighted", [D, 2, YS, F])
        w1_sb = sb("w1_sb", [P, K1, H1])
        w2_sb = sb("w2_sb", [P, K2, H2])
        w3_sb = sb("w3_sb", [P, M2])
        b1_sb = sb("b1_sb", [P, M1])
        b2_sb = sb("b2_sb", [P, M2])
        attn_wt = sb("attn_wt", [D, P])
        attn_b_sb = sb("attn_b_sb", [P, 1])
        gnn_t = sb("gnn_t", [P, B])
        pooled = sb("pooled", [D, P])
        pooled100 = sb("pooled100", [D, P])
        h1 = sb("h1", [P, M1, P])
        h2 = sb("h2", [P, M2, P])
        y_row = sb("y_row", [1, B])
        ident = sb("ident", [P, P])
        zeros = sb("zeros", [P, HALF], BF16)
        parity = sb("parity", [P, 2])
        neg_max = sb("neg_max", [P, 1])
        exp_sum = sb("exp_sum", [P, 1])
        inv_sum = sb("inv_sum", [P, 1])
        inv_par = sb("inv_par", [P, 2])
        gnn_rows = x_fields[:, 0:T, :]
        attn_w_rows = x_fields[:, T, :]

        hidden = [pb(f"hidden{i}", [P, 2, 512]) for i in range(2)]
        scores = pb("scores", [P, 2, 512])
        side = [pb(f"side{i}", [P, 512]) for i in range(2)]
        scores_v = scores[:, :, 0:HALF]

        table_rows = nc.dram_tensor("x_dram", (B, F, D), FP32, kind="Internal").ap()

        s_ids = sem("ids_loaded")
        s_ids_now = sem("ids_now_copied")
        s_gather = sem("rows_gathered")
        s_store = sem("rows_stored")
        s_fields = sem("fields_loaded")
        s_small = sem("small_inputs_loaded")
        s_weights = sem("mlp_weights_loaded")
        s_const = sem("constants_made")
        s_zero = sem("dve_zeros_made")
        s_setup_t = sem("setup_transposed")
        s_setup = sem("setup_copied")
        s_blocks = sem("gnn_blocks_written")
        s_inner = sem("inner_ready")
        s_hidden = sem("hidden_ready")
        s_fm = sem("fm_ready")
        s_red = sem("step_reduced")
        s_max = sem("max_ready")
        s_exp = sem("exp_ready")
        s_inv = sem("softmax_chain")
        s_attn = sem("attn_rows_ready")
        s_filled = {k: sem(f"{k}_filled") for k in ("attn_t", "fields", "mlp", "x_t")}
        s_emptied = {k: sem(f"{k}_emptied") for k in ("attn_t", "fields", "mlp", "x_t")}
        s_weighted = sem("weighted_ready")
        s_pooled = sem("pooled_summed")
        s_pooled100 = sem("pooled_scaled")
        s_out = sem("out_stored")
        COUNT = {"attn_t": FCH, "fields": YR, "mlp": 3, "x_t": FCH}

        block = ctx.enter_context(nc.Block())

        def tiles(eng, body):
            body(Tile(0, 0), False, True)
            with eng.Fori(0, T - 2) as loop:
                body(Tile(loop, 1), True, True)
            body(Tile(0, T - 1), True, False)

        @block.sync
        def _(sp):
            sp.dma_start(ids_all[:], ids.rearrange("(t p) f -> p t f", p=P)).then_inc(s_ids, 16)
            sp.dma_start(attn_w_rows, attn_w).then_inc(s_small, 16)
            sp.dma_start(gnn_rows, gnn.rearrange("(t p) a -> p t a", p=P)).then_inc(s_small, 16)
            sp.dma_start(attn_b_sb[:], attn_b.rearrange("(a n) -> a n", n=1), allow_slow_non_contiguous=True).then_inc(s_small, 16)
            sp.dma_start(w1_sb[:], w1.rearrange("(k p) n -> p k n", p=P)).then_inc(s_weights, 16)
            sp.dma_start(w2_sb[:], w2.rearrange("(k p) n -> p k n", p=P)).then_inc(s_weights, 16)
            sp.dma_start(w3_sb[:], w3.rearrange("(k p) n -> p (k n)", p=P), allow_slow_non_contiguous=True).then_inc(s_weights, 16)
            sp.dma_start(b1_sb[:], b1.rearrange("(m p) -> p m", p=P), allow_slow_non_contiguous=True).then_inc(s_weights, 16)
            sp.dma_start(b2_sb[:], b2.rearrange("(m p) -> p m", p=P), allow_slow_non_contiguous=True).then_inc(s_weights, 16)

            def store_rows(t):
                sp.wait_ge(s_gather, t.times(16 * F, 16 * F))
                sp.wait_ge(s_small, 48)
                sp.dma_start(table_rows[bass.ds(t.times(P), P), :, :], x_rows[:]).then_inc(s_store, 16)

            def load_fields(t, first=False):
                sp.wait_ge(s_store, t.times(16, 16))
                if first:
                    sp.wait_ge(s_setup, 3)
                else:
                    sp.wait_ge(s_filled["mlp"], t.times(3, -2))
                rows = table_rows[bass.ds(t.times(P), P), :, :].rearrange("(s q) f d -> q f s d", q=2)
                for q in ODD:
                    sp.dma_start(x_fields[q * FX:q * FX + F], rows[q]).then_inc(s_fields, 16)
                    sp.dma_start(x_fields[q * FX + F:(q + 1) * FX], rows[q, 0:K]).then_inc(s_fields, 16)

            store_rows(Tile(0, 0))
            load_fields(Tile(0, 0), first=True)
            store_rows(Tile(0, 1))
            with sp.Fori(0, T - 2) as loop:
                load_fields(Tile(loop, 1))
                store_rows(Tile(loop, 2))
            load_fields(Tile(0, T - 1))
            sp.wait_ge(s_emptied["mlp"], 3 * T)
            sp.dma_start(out.rearrange("b n -> n b"), y_row[:]).then_inc(s_out, 16)
            sp.wait_ge(s_store, 16 * T)
            sp.wait_ge(s_out, 16)

        @block.gpsimd
        def _(pool):
            def gather(t, first=False):
                if not first:
                    pool.wait_ge(s_ids_now, t.times(2))
                    pool.wait_ge(s_gather, t.times(16 * F))
                    pool.wait_ge(s_filled["x_t"], t.times(FCH))
                    pool.wait_ge(s_store, t.times(16))
                nc.gpsimd.tensor_copy(ids_now[:], ids_all[:, bass.ds(t.times(1), 1), :].rearrange("p t f -> p (t f)"))\
                    .then_inc(s_ids_now, 1)
                pool.wait_ge(s_ids_now, t.times(2, 1))
                nc.gpsimd.tensor_tensor(ids_seen[:], ids_now[:, 0:1], ids_now[:, 1:2], ALU.add).then_inc(s_ids_now, 1)
                for f in range(F):
                    nc.gpsimd.indirect_dma_start(
                        out=x_rows[:, f, :], out_offset=None, in_=tables[f],
                        in_offset=bass.IndirectOffsetOnAxis(ap=ids_now[:, f:f + 1], axis=0),
                    ).then_inc(s_gather, 16)

            pool.wait_ge(s_ids, 16)
            gather(Tile(0, 0), first=True)
            nc.gpsimd.memset(ident[:], 1.0).then_inc(s_const, 1)
            pool.wait_ge(s_const, 1)
            nc.gpsimd.affine_select(out=ident[:], in_=ident[:], compare_op=ALU.is_equal, fill=0.0, base=0,
                                    pattern=[[-1, P]], channel_multiplier=1).then_inc(s_const, 1)
            pool.wait_ge(s_const, 2)
            with pool.Fori(0, T - 1) as loop:
                gather(Tile(loop, 1))

        @block.scalar
        def _(act):
            def relus(t, s, j):
                act.wait_ge(s_hidden, t.times(P, s * GROUPS + j + 1))
                if j == 0 and not (s < 2 and t.below(1)):
                    act.wait_ge(s_red, t.times(STEPS, s - 1))
                dst = fm[:, s % 2, j * PAIRS:(j + 1) * PAIRS].rearrange("p (h n) -> p h n", h=2)
                nc.scalar.activation(dst, hidden[j % 2][:, :, 0:HALF], ACT.Relu,
                                     bias=attn_b_sb[:, 0:1]).then_inc(s_fm, 1)

            def exps(t):
                act.wait_ge(s_max, t.times(1, 1))
                dst = exp_rows[:].rearrange("p (h n) -> p h n", h=2)
                nc.scalar.activation(dst, scores_v, ACT.Exp, bias=neg_max[:, 0:1],
                                     accum_out=exp_sum[:, 0:1]).then_inc(s_exp, 1)

            def evacuate(t, job):
                kind, c = job
                if kind == "attn_t":
                    n = min(FB, F - FB * c)
                    act.wait_ge(s_filled[kind], t.times(FCH, c + 1))
                    nc.scalar.copy(attn_t[:, FB * c:FB * c + n, :],
                                   side[bank_of[job]][0:2 * FX, 0:n * P].rearrange("p (f b) -> p f b", b=P))\
                        .then_inc(s_emptied[kind], 1)
                if kind == "mlp" and c < 2:
                    m, b, h = ((M1, b1_sb, h1), (M2, b2_sb, h2))[c]
                    act.wait_ge(s_filled[kind], t.times(3, c + 1))
                    for i in range(m):
                        last = nc.scalar.activation(h[:, i, :], side[bank_of[job]][:, i * P:(i + 1) * P],
                                                    ACT.Relu, bias=b[:, i:i + 1])
                    last.then_inc(s_emptied[kind], 1)

            def tile(t, before, behind):
                for s in range(STEPS):
                    relus(t, s, 0)
                    if before and s == 1:
                        exps(t - 1)
                    if before and s > 0:
                        for job in jobs[s - 1]:
                            evacuate(t - 1, job)
                    for j in range(1, GROUPS):
                        relus(t, s, j)

            act.wait_ge(s_small, 48)
            act.wait_ge(s_weights, 80)
            tiles(act, tile)
            exps(Tile(0, T - 1))
            for s in range(STEPS):
                for job in jobs[s]:
                    evacuate(Tile(0, T - 1), job)

        @block.vector
        def _(dve):
            def product(t, s):
                if not (t.below(1) and s < 2):
                    dve.wait_ge(s_hidden, t.times(P, (s - 1) * GROUPS))
                x = xt[:, bass.ds(t.odd(), 1), s:(GROUPS - 1) * STEPS + s + 1:STEPS, :]\
                    .rearrange("d o g f -> d (o g) f")
                lo = x[:, :, 0:F]
                part, sample, field = lo.ap
                lo = bass.AP(tensor=lo.tensor, offset=lo.offset, ap=[part, sample, [0, K], field])
                hi = x[:, :, 1:1 + F]
                hi = bass.AP(tensor=hi.tensor, offset=hi.offset, ap=[part, sample, [1, K], field])
                dst = inner[:, s % 2, :].rearrange("d (g k f) -> d g k f", g=GROUPS, k=K)
                nc.vector.tensor_tensor(dst, lo, hi, ALU.mult).then_inc(s_inner, 1)

            def gnn_block(t):
                b = gnn_blocks[:].rearrange("a g s c -> a g (s c)")
                dst = b[:, :, 0:(STEPS - 1) * (STEPS + 1) + 1:STEPS + 1]
                src = gnn_t[:, bass.ds(t.times(P), P)].rearrange("a (g s) -> a g s", g=GROUPS)
                nc.vector.tensor_scalar(dst, src, 1.0, None, ALU.mult).then_inc(s_blocks, 1)

            def row_max(t):
                dve.wait_ge(s_red, (t + 1).times(STEPS))
                nc.vector.tensor_reduce(neg_max[:, 0:1], scores_v, AX.XY, ALU.max, negate=True)\
                    .then_inc(s_max, 1)

            def attn(t):
                dve.wait_ge(s_exp, t.times(1, 1))
                nc.vector.reciprocal(inv_sum[:, 0:1], exp_sum[:, 0:1]).then_inc(s_inv, 1)
                dve.wait_ge(s_inv, t.times(2, 1))
                nc.vector.tensor_scalar(inv_par[:], parity[:], inv_sum[:, 0:1], None, ALU.mult)\
                    .then_inc(s_inv, 1)
                dve.wait_ge(s_inv, t.times(2, 2))
                for q in ODD:
                    first = attn_rows[:, q * FX + 1:q * FX + 2]
                    dst = bass.AP(tensor=first.tensor, offset=first.offset,
                                  ap=[first.ap[0], [1, K], [2 * FX + 1, F]])
                    last = nc.vector.tensor_scalar(dst, exp_rows[:].rearrange("p (k i) -> p k i", k=K),
                                                   inv_par[:, q:q + 1], None, ALU.mult)
                last.then_inc(s_attn, 1)

            def evacuate_x(t, c):
                n = min(FB, F - FB * c)
                dve.wait_ge(s_filled["x_t"], t.times(FCH, c + 1))
                src = side[bank_of[("x_t", c)]][:, 0:n * P].rearrange("d (f b) -> d f b", b=P)
                for at in (0, F)[:1 + (FB * c < K)]:
                    dst = xt[:, bass.ds(t.odd(), 1), :, at + FB * c:at + FB * c + n]\
                        .rearrange("d o b f -> d f (o b)")
                    last = nc.vector.tensor_scalar(dst, src, 1.0, None, ALU.mult)
                last.then_inc(s_emptied["x_t"], 1)

            def weigh(t, r):
                w = weighted[:, r % 2, :, :]
                dve.wait_ge(s_filled["fields"], t.times(YR, r + 1))
                x = xt[:, bass.ds(t.odd(), 1), YS * r:YS * r + YS, 0:F].rearrange("d o b f -> d (o b) f")
                y = side[bank_of[("fields", r)]][:, 0:YS * F].rearrange("d (b f) -> d b f", f=F)
                nc.vector.tensor_tensor(w, y, x, ALU.mult).then_inc(s_weighted, 1)
                if r > 0:
                    dve.wait_ge(s_pooled, t.times(YR, r))
                dve.wait_ge(s_weighted, t.times(YR, r + 1))
                nc.vector.tensor_reduce(pooled[:, YS * r:YS * r + YS], w, AX.X, ALU.add)\
                    .then_inc(s_pooled, 1)
                if r == YR - 1:
                    dve.wait_ge(s_pooled, t.times(YR, YR))
                    nc.vector.tensor_scalar(pooled100[:], pooled[:], 100.0, None, ALU.mult)\
                        .then_inc(s_pooled100, 1)

            def evacuate(t, job):
                kind, c = job
                if kind == "fields":
                    weigh(t, c)
                if kind == "mlp" and c == 2:
                    dve.wait_ge(s_filled[kind], t.times(3, 3))
                    nc.vector.tensor_scalar(y_row[0:1, bass.ds(t.times(P), P)], side[bank_of[job]][0:1, 0:P],
                                            1.0, None, ALU.mult).then_inc(s_emptied[kind], 1)

            def tile(t, before, behind):
                for s in range(STEPS):
                    if before and s == 0:
                        row_max(t - 1)
                        gnn_block(t)
                    if s < STEPS - 2:
                        product(t, s + 2)
                    elif behind:
                        if s == STEPS - 2:
                            dve.wait_ge(s_emptied["x_t"], (t + 2).times(FCH))
                        product(t + 1, s + 2 - STEPS)
                    if before and s == 1:
                        attn(t - 1)
                    for job in jobs[s]:
                        if job[0] == "x_t" and behind:
                            evacuate_x(t + 1, job[1])
                        if job[0] != "x_t" and before:
                            evacuate(t - 1, job)

            nc.vector.memset(gnn_blocks[:], 0.0).then_inc(s_zero, 1)
            nc.vector.memset(attn_rows[:], 0.0).then_inc(s_zero, 1)
            nc.vector.memset(zeros[:], 0.0).then_inc(s_zero, 1)
            dve.wait_ge(s_const, 2)
            nc.vector.tensor_reduce(parity[:], ident[:].rearrange("p (n q) -> p q n", q=2), AX.X, ALU.add)\
                .then_inc(s_zero, 1)
            for n in range(2):
                dve.wait_ge(s_setup_t, n + 1)
                nc.vector.tensor_copy(gnn_t[:, n * 4 * P:(n + 1) * 4 * P], side[n][:]).then_inc(s_setup, 1)
            dve.wait_ge(s_setup_t, 3)
            nc.vector.tensor_copy(attn_wt[:], side[0][:, 0:P]).then_inc(s_setup, 1)
            dve.wait_ge(s_zero, 4)
            dve.wait_ge(s_setup, 2)
            gnn_block(Tile(0, 0))
            for c in range(FCH):
                evacuate_x(Tile(0, 0), c)
            dve.wait_ge(s_emptied["x_t"], FCH)
            product(Tile(0, 0), 0)
            product(Tile(0, 0), 1)
            tiles(dve, tile)
            row_max(Tile(0, T - 1))
            attn(Tile(0, T - 1))
            for s in range(STEPS):
                for job in jobs[s]:
                    evacuate(Tile(0, T - 1), job)

        @block.tensor
        def _(pe):
            def hidden_of(t, s):
                pe.wait_ge(s_inner, t.times(STEPS, s + 1))
                for j in range(GROUPS):
                    if not (t.below(1) and s == 0 and j < 2):
                        pe.wait_ge(s_fm, t.times(P, s * GROUPS + j - 1))
                    for h in range(2):
                        at = j * PAIRS + h * HALF
                        last = nc.tensor.matmul(hidden[j % 2][:, h, 0:HALF], attn_wt[:],
                                                inner[:, s % 2, at:at + HALF], start=True, stop=True)
                    last.then_inc(s_hidden, 1)

            def open_scores(t):
                if not t.below(1):
                    pe.wait_ge(s_exp, t.times(1))
                for h in range(2):
                    nc.tensor.matmul(scores[:, h, 0:HALF], zeros[:, 0:P], zeros[:], start=True, stop=False,
                                     skip_group_check=True)

            def reduce_step(t, s):
                if s == 0:
                    open_scores(t)
                    pe.wait_ge(s_blocks, t.times(1, 1))
                pe.wait_ge(s_fm, t.times(P, (s + 1) * GROUPS))
                for h in range(2):
                    for j in range(GROUPS):
                        at = j * PAIRS + h * HALF
                        last = nc.tensor.matmul(scores[32 * j:32 * j + 32, h, 0:HALF], gnn_blocks[:, j, s, :],
                                                fm[:, s % 2, at:at + HALF], start=False, stop=s == STEPS - 1,
                                                skip_group_check=True)
                last.then_inc(s_red, 1)

            def transpose_x(t, c):
                bank = side[bank_of[("x_t", c)]]
                if c == 0:
                    pe.wait_ge(s_gather, t.times(16 * F, 16 * F))
                    if not t.below(2):
                        pe.wait_ge(s_emptied["mlp"], (t - 1).times(3))
                if c >= 2:
                    pe.wait_ge(s_emptied["x_t"], t.times(FCH, c - 1))
                for n in range(min(FB, F - FB * c)):
                    last = nc.tensor.transpose(bank[:, n * P:(n + 1) * P], x_rows[:, FB * c + n, :], ident[:])
                last.then_inc(s_filled["x_t"], 1)

            def work(t, job, last_tile=False):
                kind, c = job
                bank = side[bank_of[job]]
                if kind == "attn_t":
                    if c == 0:
                        pe.wait_ge(s_attn, t.times(1, 1))
                        if last_tile:
                            pe.wait_ge(s_emptied["mlp"], t.times(3))
                        else:
                            pe.wait_ge(s_emptied["x_t"], (t + 2).times(FCH))
                    if c >= 2:
                        pe.wait_ge(s_emptied[kind], t.times(FCH, c - 1))
                    cols = attn_rows[:].rearrange("p (i c) -> p i c", i=F)
                    for n in range(min(FB, F - FB * c)):
                        last = nc.tensor.transpose(bank[0:2 * FX, n * P:(n + 1) * P], cols[:, FB * c + n, :],
                                                   ident[:])
                    last.then_inc(s_filled[kind], 1)
                if kind == "fields":
                    if c < 2:
                        pe.wait_ge(s_emptied["attn_t"], (t + 1).times(FCH))
                    else:
                        pe.wait_ge(s_weighted, t.times(YR, c - 1))
                    if c == 0:
                        pe.wait_ge(s_fields, (t + 1).times(64))
                    for n in range(YS // 2):
                        pair = c * (YS // 2) + n
                        rhs = attn_t[:, :, 2 * pair:2 * pair + 2].rearrange("p i b -> p b i")
                        last = nc.tensor.matmul(bank[:, n * 2 * F:(n + 1) * 2 * F], x_fields[0:2 * FX, pair, :],
                                                rhs, start=True, stop=True)
                    last.then_inc(s_filled[kind], 1)
                if kind == "mlp" and c == 0:
                    pe.wait_ge(s_weighted, (t + 1).times(YR))
                    pe.wait_ge(s_pooled100, t.times(1, 1))
                    g = gnn_t[:, bass.ds(t.times(P), P)]
                    for m in range(M1):
                        for k, z in enumerate((g, pooled100[:], g)):
                            last = nc.tensor.matmul(bank[:, m * P:(m + 1) * P], w1_sb[:, k, m * P:(m + 1) * P], z,
                                                    start=k == 0, stop=k == K1 - 1)
                    last.then_inc(s_filled[kind], 1)
                if kind == "mlp" and c == 1:
                    pe.wait_ge(s_emptied[kind], t.times(3, 1))
                    for m in range(M2):
                        for k in range(K2):
                            last = nc.tensor.matmul(bank[:, m * P:(m + 1) * P], w2_sb[:, k, m * P:(m + 1) * P],
                                                    h1[:, k, :], start=k == 0, stop=k == K2 - 1)
                    last.then_inc(s_filled[kind], 1)
                if kind == "mlp" and c == 2:
                    pe.wait_ge(s_emptied[kind], t.times(3, 2))
                    for k in range(M2):
                        last = nc.tensor.matmul(bank[0:1, 0:P], w3_sb[:, k:k + 1], h2[:, k, :],
                                                start=k == 0, stop=k == M2 - 1)
                    last.then_inc(s_filled[kind], 1)

            def tile(t, before, behind):
                for s in range(STEPS):
                    hidden_of(t, s)
                    if s > 0:
                        reduce_step(t, s - 1)
                    elif before:
                        reduce_step(t - 1, STEPS - 1)
                    for job in jobs[s]:
                        if job[0] == "x_t" and behind:
                            transpose_x(t + 1, job[1])
                        if job[0] != "x_t" and before:
                            work(t - 1, job)

            pe.wait_ge(s_const, 2)
            pe.wait_ge(s_small, 48)
            for n in range(2):
                for i in range(4):
                    last = nc.tensor.transpose(side[n][:, i * P:(i + 1) * P], gnn_rows[:, n * 4 + i, :], ident[:])
                last.then_inc(s_setup_t, 1)
            pe.wait_ge(s_setup, 1)
            nc.tensor.transpose(side[0][:, 0:P], attn_w_rows, ident[:]).then_inc(s_setup_t, 1)
            pe.wait_ge(s_setup, 3)
            pe.wait_ge(s_weights, 80)
            for c in range(FCH):
                transpose_x(Tile(0, 0), c)
            pe.wait_ge(s_zero, 4)
            tiles(pe, tile)
            reduce_step(Tile(0, T - 1), STEPS - 1)
            for s in range(STEPS):
                for job in jobs[s]:
                    if job[0] != "x_t":
                        work(Tile(0, T - 1), job, last_tile=True)


def kernel(**inputs):
    import numpy as _np
    import concourse.bacc as _bacc
    from concourse import mybir as _mybir
    from concourse.bass_utils import run_bass_kernel_spmd as _run

    nc = _bacc.Bacc("TRN2", target_bir_lowering=False, num_devices=1)
    arrays = {}

    def given(name):
        a = _np.ascontiguousarray(inputs[name])
        arrays[f"in_{name}"] = a
        return nc.dram_tensor(f"in_{name}", a.shape, _mybir.dt.from_np(a.dtype), kind="ExternalInput").ap()

    fields = inputs["ids"].shape[1]
    args = [given("r_gnn_feature"), given("ids"), [given(f"tbl_{f}") for f in range(fields)]]
    args += [given(n) for n in ("W_top1", "b_top1", "W_top2", "b_top2", "W_top3", "L0_rec_attn_W", "L0_rec_attn_b")]
    out = nc.dram_tensor("out_y", (inputs["ids"].shape[0], 1), FP32, kind="ExternalOutput").ap()
    afm_tower(nc, *args, out)
    r = _run(nc, [arrays], core_ids=[0])
    return r.results[0]["out_y"]
```

```python
import concourse.bass as bass
from concourse import mybir
from contextlib import ExitStack

FP32 = mybir.dt.float32
FP32R = mybir.dt.float32r
BF16 = mybir.dt.bfloat16
I32 = mybir.dt.int32
ALU = mybir.AluOpType
ACT = mybir.ActivationFunctionType
AX = mybir.AxisListType


class Tile:

    def __init__(self, loop, ahead):
        self.loop, self.ahead = loop, ahead

    def __add__(self, n):
        return Tile(self.loop, self.ahead + n)

    def __sub__(self, n):
        return Tile(self.loop, self.ahead - n)

    def times(self, each, more=0):
        if isinstance(self.loop, int):
            return (self.loop + self.ahead) * each + more
        return self.loop * each + (self.ahead * each + more)

    def odd(self):
        return (self.loop + self.ahead) % 2

    def below(self, n):
        return isinstance(self.loop, int) and self.loop + self.ahead < n


def afm_tower(nc, gnn, ids, tables, w1, b1, w2, b2, w3, attn_w, attn_b, out):
    P = 128
    B, D = gnn.shape
    F = len(tables)
    T = B // P
    K = (F - 1) // 2
    FX = F + K
    PAIRS = K * F
    HALF = PAIRS // 2
    GROUPS = 4
    STEPS = P // GROUPS
    H1, H2 = w1.shape[1], w2.shape[1]
    K1, M1, K2, M2 = w1.shape[0] // P, H1 // P, H2 and H1 // P, H2 // P
    NATIVE = 1
    SPLIT = GROUPS - NATIVE
    FB = 4
    FU = 2 * FB
    FUNITS = -(-F // FU)
    YB = 8
    YS = 2 * YB
    YR = P // YS
    FIELD_BUFS = 3
    ODD = range(2)

    jobs = {s: [] for s in range(STEPS)}
    for c in range(FUNITS):
        jobs[2 + c].append(("attn_t", c))
        jobs[STEPS - 5 - FUNITS + c].append(("x_t", c))
    for n in range(YR):
        jobs[2 + FUNITS + n].append(("fields", n))
    for n in range(3):
        jobs[3 + FUNITS + YR + 2 * n].append(("mlp", n))
    COUNT = {"attn_t": FUNITS, "fields": YR, "mlp": 3, "x_t": FUNITS}
    RING = 3
    units = []
    for s in range(STEPS):
        if s == STEPS - 1:
            units += [None] * (-(len(units) + GROUPS) % RING)
        units += [("sample", s * GROUPS + j) for j in range(GROUPS)] + jobs[s]
    place = {u: n for n, u in enumerate(units) if u}

    ctx = ExitStack()
    with ctx:
        def sb(name, shape, dt=FP32):
            return ctx.enter_context(nc.sbuf_tensor(name, shape, dt))

        def pb(name, shape):
            return ctx.enter_context(nc.psum_tensor(name, shape, FP32))

        def sem(name):
            return ctx.enter_context(nc.semaphore(name))

        ids_all = sb("ids_all", [P, T, F], I32)
        ids_now = sb("ids_now", [P, F], I32)
        ids_seen = sb("ids_seen", [P, 1], I32)
        x_rows = sb("x_rows", [P, F, D])
        xt = sb("xt", [D, 2, P, FX])
        inner = sb("inner", [D, 2, GROUPS * PAIRS])
        inner_hi = sb("inner_hi", [D, 2, SPLIT * PAIRS], FP32R)
        inner_lo = sb("inner_lo", [D, 2, SPLIT * PAIRS], FP32R)
        fm = sb("fm", [P, 2, GROUPS * PAIRS])
        gnn_blocks = sb("gnn_blocks", [P, GROUPS, STEPS, STEPS])
        x_fields = sb("x_fields", [P, FIELD_BUFS, YS // 2, D])
        attn_rows = sb("attn_rows", [P, F * 2 * FX])
        exp_rows = sb("exp_rows", [P, PAIRS])
        attn_t = sb("attn_t", [2 * FX, F, P])
        weighted = sb("weighted", [D, YS, F])
        w1_sb = sb("w1_sb", [P, K1, H1])
        w2_sb = sb("w2_sb", [P, K2, H2])
        w3_sb = sb("w3_sb", [P, M2])
        b1_sb = sb("b1_sb", [P, M1])
        b2_sb = sb("b2_sb", [P, M2])
        attn_wt = sb("attn_wt", [D, P])
        attn_wt_hi = sb("attn_wt_hi", [D, P], FP32R)
        attn_wt_lo = sb("attn_wt_lo", [D, P], FP32R)
        attn_b_sb = sb("attn_b_sb", [P, 1])
        gnn_t = sb("gnn_t", [P, B])
        pooled = sb("pooled", [D, P])
        pooled100 = sb("pooled100", [D, P])
        h1 = sb("h1", [P, M1, P])
        h2 = sb("h2", [P, M2, P])
        y_row = sb("y_row", [1, P])
        ident = sb("ident", [P, P])
        zeros = sb("zeros", [P, HALF], BF16)
        parity = sb("parity", [P, 2])
        neg_max = sb("neg_max", [P, 1])
        exp_sum = sb("exp_sum", [P, 1])
        inv_sum = sb("inv_sum", [P, 1])
        inv_par = sb("inv_par", [P, 2])
        gnn_rows = x_fields[:, 0, 0:T, :]
        attn_w_rows = x_fields[:, 1, 0, :]

        ring = [pb(f"ring{i}", [P, 2, 512]) for i in range(RING)]
        scores = pb("scores", [P, 2, 512])

        def banks(unit):
            return ring[place[unit] % RING]

        scores_v = scores[:, :, 0:HALF]

        table_rows = nc.dram_tensor("x_dram", (B, F, D), FP32, kind="Internal").ap()

        s_ids = sem("ids_loaded")
        s_ids_now = sem("ids_now_copied")
        s_gather = [sem(f"rows_gathered{c}") for c in range(FUNITS)]
        s_store = sem("rows_stored")
        s_fields = [sem(f"fields_loaded{i}") for i in range(FIELD_BUFS)]
        s_small = sem("small_inputs_loaded")
        s_weights = sem("mlp_weights_loaded")
        s_const = sem("constants_made")
        s_zero = sem("dve_zeros_made")
        s_setup_t = sem("setup_transposed")
        s_setup = sem("setup_copied")
        s_blocks = sem("gnn_blocks_written")
        s_inner = sem("split_inner_ready")
        s_native = sem("native_inner_ready")
        s_hi = sem("inner_hi_ready")
        s_lo = sem("inner_lo_ready")
        s_hidden = sem("hidden_ready")
        s_fm = sem("fm_ready")
        s_red = sem("step_reduced")
        s_max = sem("max_ready")
        s_exp = sem("exp_ready")
        s_inv = sem("softmax_chain")
        s_attn = sem("attn_rows_ready")
        s_filled = {k: sem(f"{k}_filled") for k in ("attn_t", "fields", "mlp", "x_t")}
        s_emptied = {k: sem(f"{k}_emptied") for k in ("attn_t", "fields", "mlp", "x_t")}
        s_weighted = sem("weighted_ready")
        s_pooled = sem("pooled_summed")
        s_pooled100 = sem("pooled_scaled")
        s_out = sem("out_stored")

        def rows_here(eng, t, units):
            for c in units:
                n = 16 * min(FU, F - FU * c)
                eng.wait_ge(s_gather[c], t.times(n, n))

        def taken_out(t, unit):
            kind, n = unit
            if kind == "sample":
                return s_fm, t.times(P, n + 1)
            if kind == "fields":
                return s_weighted, t.times(YR, n + 1)
            return s_emptied[kind], t.times(COUNT[kind], n + 1)

        block = ctx.enter_context(nc.Block())

        def step(t, s):
            return (t, s) if s < STEPS else (t + 1, s - STEPS)

        def tiles(eng, body):
            body(Tile(0, 0), False, True)
            with eng.Fori(0, T - 2) as loop:
                body(Tile(loop, 1), True, True)
            body(Tile(0, T - 1), True, False)

        @block.sync
        def _(sp):
            sp.dma_start(ids_all[:], ids.rearrange("(t p) f -> p t f", p=P)).then_inc(s_ids, 16)
            sp.dma_start(attn_w_rows, attn_w).then_inc(s_small, 16)
            sp.dma_start(gnn_rows, gnn.rearrange("(t p) a -> p t a", p=P)).then_inc(s_small, 16)
            sp.dma_start(attn_b_sb[:], attn_b.rearrange("(a n) -> a n", n=1), allow_slow_non_contiguous=True).then_inc(s_small, 16)
            sp.dma_start(w1_sb[:], w1.rearrange("(k p) n -> p k n", p=P)).then_inc(s_weights, 16)
            sp.dma_start(w2_sb[:], w2.rearrange("(k p) n -> p k n", p=P)).then_inc(s_weights, 16)
            sp.dma_start(w3_sb[:], w3.rearrange("(k p) n -> p (k n)", p=P), allow_slow_non_contiguous=True).then_inc(s_weights, 16)
            sp.dma_start(b1_sb[:], b1.rearrange("(m p) -> p m", p=P), allow_slow_non_contiguous=True).then_inc(s_weights, 16)
            sp.dma_start(b2_sb[:], b2.rearrange("(m p) -> p m", p=P), allow_slow_non_contiguous=True).then_inc(s_weights, 16)

            def store_rows(t):
                sp.wait_ge(s_filled["x_t"], t.times(FUNITS, FUNITS))
                sp.dma_start(table_rows[bass.ds(t.times(P), P), :, :], x_rows[:]).then_inc(s_store, 16)

            def load_fields(t, r):
                rows = table_rows[bass.ds(t.times(P, r * YS), YS), :, :].rearrange("(s q) f d -> q f s d", q=2)
                to = x_fields[:, r % FIELD_BUFS, :, :]
                for q in ODD:
                    sp.dma_start(to[q * FX:q * FX + F], rows[q]).then_inc(s_fields[r % FIELD_BUFS], 16)
                    sp.dma_start(to[q * FX + F:(q + 1) * FX], rows[q, 0:K]).then_inc(s_fields[r % FIELD_BUFS], 16)

            def after(t, store):
                for r in range(YR):
                    if r == 0:
                        sp.wait_ge(s_store, t.times(16, 16))
                    if r < FIELD_BUFS and not t.below(1):
                        last = [n for n in range(YR) if n % FIELD_BUFS == r][-1]
                        sp.wait_ge(s_filled["fields"], t.times(YR, last + 1 - YR))
                    if r >= FIELD_BUFS:
                        sp.wait_ge(s_filled["fields"], t.times(YR, r - FIELD_BUFS + 1))
                    load_fields(t, r)
                if store:
                    store_rows(t + 2)

            store_rows(Tile(0, 0))
            store_rows(Tile(0, 1))
            sp.wait_ge(s_setup, 3)
            after(Tile(0, 0), True)
            with sp.Fori(0, T - 3) as loop:
                after(Tile(loop, 1), True)
            after(Tile(0, T - 2), False)
            after(Tile(0, T - 1), False)
            sp.wait_ge(s_store, 16 * T)
            sp.wait_ge(s_out, 16 * T)

        @block.gpsimd
        def _(pool):
            def gather(t, first=False):
                if not first:
                    pool.wait_ge(s_ids_now, t.times(2))
                    rows_here(pool, t - 1, range(FUNITS))
                    pool.wait_ge(s_filled["x_t"], t.times(FUNITS))
                    pool.wait_ge(s_store, t.times(16))
                nc.gpsimd.tensor_copy(ids_now[:], ids_all[:, bass.ds(t.times(1), 1), :].rearrange("p t f -> p (t f)"))\
                    .then_inc(s_ids_now, 1)
                pool.wait_ge(s_ids_now, t.times(2, 1))
                nc.gpsimd.tensor_tensor(ids_seen[:], ids_now[:, 0:1], ids_now[:, 1:2], ALU.add).then_inc(s_ids_now, 1)
                for f in range(F):
                    nc.gpsimd.indirect_dma_start(
                        out=x_rows[:, f, :], out_offset=None, in_=tables[f],
                        in_offset=bass.IndirectOffsetOnAxis(ap=ids_now[:, f:f + 1], axis=0),
                    ).then_inc(s_gather[f // FU], 16)

            nc.gpsimd.memset(ident[:], 1.0).then_inc(s_const, 1)
            pool.wait_ge(s_const, 1)
            nc.gpsimd.affine_select(out=ident[:], in_=ident[:], compare_op=ALU.is_equal, fill=0.0, base=0,
                                    pattern=[[-1, P]], channel_multiplier=1).then_inc(s_const, 1)
            pool.wait_ge(s_const, 2)
            pool.wait_ge(s_ids, 16)
            gather(Tile(0, 0), first=True)
            with pool.Fori(0, T - 1) as loop:
                gather(Tile(loop, 1))

        @block.scalar
        def _(act):
            def relus(t, s, j):
                act.wait_ge(s_hidden, t.times(P, s * GROUPS + j + 1))
                if j == 0 and not (s < 2 and t.below(1)):
                    act.wait_ge(s_red, t.times(STEPS, s - 1))
                dst = fm[:, s % 2, j * PAIRS:(j + 1) * PAIRS].rearrange("p (h n) -> p h n", h=2)
                nc.scalar.activation(dst, banks(("sample", s * GROUPS + j))[:, :, 0:HALF], ACT.Relu,
                                     bias=attn_b_sb[:, 0:1]).then_inc(s_fm, 1)

            def round_inner(t, s):
                act.wait_ge(s_inner, t.times(STEPS, s + 1))
                if not (t.below(1) and s < 2):
                    act.wait_ge(s_hidden, t.times(P, (s - 1) * GROUPS))
                nc.scalar.copy(inner_hi[:, s % 2, :], inner[:, s % 2, NATIVE * PAIRS:]).then_inc(s_hi, 1)

            def exps(t):
                act.wait_ge(s_max, t.times(1, 1))
                dst = exp_rows[:].rearrange("p (h n) -> p h n", h=2)
                nc.scalar.activation(dst, scores_v, ACT.Exp, bias=neg_max[:, 0:1],
                                     accum_out=exp_sum[:, 0:1]).then_inc(s_exp, 1)

            def evacuate(t, job):
                kind, c = job
                src = banks(job)
                act.wait_ge(s_filled[kind], t.times(COUNT[kind], c + 1))
                if kind in ("attn_t", "x_t"):
                    n = min(FU, F - FU * c)
                    h = -(-n // FB)
                    src = src[:, 0:h, 0:min(n, FB) * P].rearrange("p h (f b) -> p (h f) b", b=P)
                if kind == "attn_t":
                    last = nc.scalar.copy(attn_t[:, FU * c:FU * c + n, :], src[0:2 * FX])
                if kind == "x_t":
                    for at in (0, F)[:1 + (FU * c < K)]:
                        dst = xt[:, bass.ds(t.odd(), 1), :, at + FU * c:at + FU * c + n]\
                            .rearrange("d o b f -> d f (o b)")
                        last = nc.scalar.copy(dst, src)
                if kind == "mlp" and c < 2:
                    m, b, h = ((M1, b1_sb, h1), (M2, b2_sb, h2))[c]
                    for i in range(m):
                        last = nc.scalar.activation(h[:, i, :], src[:, 0, i * P:(i + 1) * P],
                                                    ACT.Relu, bias=b[:, i:i + 1])
                if kind == "mlp" and c == 2:
                    if not t.below(1):
                        act.wait_ge(s_out, t.times(16))
                    last = nc.scalar.copy(y_row[:], src[0:1, 0, 0:P])
                last.then_inc(s_emptied[kind], 1)
                if kind == "mlp" and c == 2:
                    act.wait_ge(s_emptied[kind], t.times(3, 3))
                    act.dma_start(out[bass.ds(t.times(P), P), :].rearrange("b n -> n b"), y_row[:]).then_inc(s_out, 16)

            def tile(t, before, behind):
                for s in range(STEPS):
                    relus(t, s, 0)
                    if before and s == 1:
                        exps(t - 1)
                    for j in range(1, GROUPS):
                        relus(t, s, j)
                    if s < STEPS - 2 or behind:
                        round_inner(*step(t, s + 2))
                    for job in jobs[s]:
                        if job[0] == "x_t" and behind:
                            evacuate(t + 1, job)
                        if job[0] in ("attn_t", "mlp") and before:
                            evacuate(t - 1, job)

            act.wait_ge(s_small, 48)
            act.wait_ge(s_weights, 80)
            act.wait_ge(s_setup, 3)
            nc.scalar.copy(attn_wt_hi[:], attn_wt[:]).then_inc(s_setup, 1)
            for c in range(FUNITS):
                evacuate(Tile(0, 0), ("x_t", c))
            for s in range(2):
                round_inner(Tile(0, 0), s)
            tiles(act, tile)
            exps(Tile(0, T - 1))
            for s in range(STEPS):
                for job in jobs[s]:
                    if job[0] in ("attn_t", "mlp"):
                        evacuate(Tile(0, T - 1), job)

        @block.vector
        def _(dve):
            def product(t, s, first, n):
                x = xt[:, bass.ds(t.odd(), 1), first * STEPS + s:(first + n - 1) * STEPS + s + 1:STEPS, :]\
                    .rearrange("d o g f -> d (o g) f")
                lo = x[:, :, 0:F]
                part, sample, field = lo.ap
                lo = bass.AP(tensor=lo.tensor, offset=lo.offset, ap=[part, sample, [0, K], field])
                hi = x[:, :, 1:1 + F]
                hi = bass.AP(tensor=hi.tensor, offset=hi.offset, ap=[part, sample, [1, K], field])
                dst = inner[:, s % 2, first * PAIRS:(first + n) * PAIRS]
                return nc.vector.tensor_tensor(dst.rearrange("d (g k f) -> d g k f", g=n, k=K), lo, hi, ALU.mult)

            def split_product(t, s):
                if not (t.below(1) and s < 2):
                    dve.wait_ge(s_lo, t.times(STEPS, s - 1))
                product(t, s, NATIVE, SPLIT).then_inc(s_inner, 1)

            def native_product(t, s):
                if not (t.below(1) and s < 2):
                    dve.wait_ge(s_hidden, t.times(P, (s - 2) * GROUPS + NATIVE))
                product(t, s, 0, NATIVE).then_inc(s_native, 1)

            def rest_of_inner(t, s):
                dve.wait_ge(s_hi, t.times(STEPS, s + 1))
                nc.vector.tensor_tensor(inner_lo[:, s % 2, :], inner[:, s % 2, NATIVE * PAIRS:],
                                        inner_hi[:, s % 2, :].bitcast(FP32), ALU.subtract).then_inc(s_lo, 1)

            def gnn_block(t):
                b = gnn_blocks[:].rearrange("a g s c -> a g (s c)")
                dst = b[:, :, 0:(STEPS - 1) * (STEPS + 1) + 1:STEPS + 1]
                src = gnn_t[:, bass.ds(t.times(P), P)].rearrange("a (g s) -> a g s", g=GROUPS)
                nc.vector.tensor_scalar(dst, src, 1.0, None, ALU.mult).then_inc(s_blocks, 1)

            def row_max(t):
                dve.wait_ge(s_red, (t + 1).times(STEPS))
                nc.vector.tensor_reduce(neg_max[:, 0:1], scores_v, AX.XY, ALU.max, negate=True)\
                    .then_inc(s_max, 1)

            def attn(t):
                dve.wait_ge(s_exp, t.times(1, 1))
                nc.vector.reciprocal(inv_sum[:, 0:1], exp_sum[:, 0:1]).then_inc(s_inv, 1)
                dve.wait_ge(s_inv, t.times(2, 1))
                nc.vector.tensor_scalar(inv_par[:], parity[:], inv_sum[:, 0:1], None, ALU.mult)\
                    .then_inc(s_inv, 1)
                dve.wait_ge(s_inv, t.times(2, 2))
                for q in ODD:
                    first = attn_rows[:, q * FX + 1:q * FX + 2]
                    dst = bass.AP(tensor=first.tensor, offset=first.offset,
                                  ap=[first.ap[0], [1, K], [2 * FX + 1, F]])
                    last = nc.vector.tensor_scalar(dst, exp_rows[:].rearrange("p (k i) -> p k i", k=K),
                                                   inv_par[:, q:q + 1], None, ALU.mult)
                last.then_inc(s_attn, 1)

            def weigh(t, r):
                dve.wait_ge(s_filled["fields"], t.times(YR, r + 1))
                x = xt[:, bass.ds(t.odd(), 1), YS * r:YS * r + YS, 0:F].rearrange("d o (h b) f -> d (o h) b f", h=2)
                y = banks(("fields", r))[:, :, 0:YB * F].rearrange("d h (b f) -> d h b f", f=F)
                w = weighted[:].rearrange("d (h b) f -> d h b f", h=2)
                nc.vector.tensor_tensor(w, y, x, ALU.mult).then_inc(s_weighted, 1)
                dve.wait_ge(s_weighted, t.times(YR, r + 1))
                nc.vector.tensor_reduce(pooled[:, YS * r:YS * r + YS], weighted[:], AX.X, ALU.add)\
                    .then_inc(s_pooled, 1)
                dve.wait_ge(s_pooled, t.times(YR, r + 1))
                if r == YR - 1:
                    nc.vector.tensor_scalar(pooled100[:], pooled[:], 100.0, None, ALU.mult)\
                        .then_inc(s_pooled100, 1)

            def tile(t, before, behind):
                for s in range(STEPS):
                    if s == STEPS - 2 and behind:
                        dve.wait_ge(s_emptied["x_t"], (t + 2).times(FUNITS))
                    if s < STEPS - 2 or behind:
                        split_product(*step(t, s + 2))
                    if s < STEPS - 1 or behind:
                        rest_of_inner(*step(t, s + 1))
                    if s < STEPS - 2 or behind:
                        native_product(*step(t, s + 2))
                    if before and s == 0:
                        row_max(t - 1)
                        gnn_block(t)
                    if before and s == 1:
                        attn(t - 1)
                    for job in jobs[s]:
                        if job[0] == "fields" and before:
                            weigh(t - 1, job[1])

            nc.vector.memset(gnn_blocks[:], 0.0).then_inc(s_zero, 1)
            nc.vector.memset(attn_rows[:], 0.0).then_inc(s_zero, 1)
            nc.vector.memset(zeros[:], 0.0).then_inc(s_zero, 1)
            dve.wait_ge(s_const, 2)
            nc.vector.tensor_reduce(parity[:], ident[:].rearrange("p (n q) -> p q n", q=2), AX.X, ALU.add)\
                .then_inc(s_zero, 1)
            dve.wait_ge(s_setup_t, 1)
            nc.vector.tensor_copy(gnn_t[:].rearrange("a (h b) -> a h b", h=2), ring[0][:]).then_inc(s_setup, 1)
            dve.wait_ge(s_setup_t, 2)
            nc.vector.tensor_copy(attn_wt[:], ring[1][:, 0, 0:P]).then_inc(s_setup, 2)
            dve.wait_ge(s_setup, 4)
            nc.vector.tensor_tensor(attn_wt_lo[:], attn_wt[:], attn_wt_hi[:].bitcast(FP32), ALU.subtract)\
                .then_inc(s_setup, 1)
            dve.wait_ge(s_zero, 4)
            dve.wait_ge(s_weights, 80)
            nc.vector.tensor_tensor(w1_sb[:, 0, :], w1_sb[:, 0, :], w1_sb[:, 2, :], ALU.add).then_inc(s_setup, 1)
            gnn_block(Tile(0, 0))
            dve.wait_ge(s_emptied["x_t"], FUNITS)
            split_product(Tile(0, 0), 0)
            native_product(Tile(0, 0), 0)
            rest_of_inner(Tile(0, 0), 0)
            split_product(Tile(0, 0), 1)
            native_product(Tile(0, 0), 1)
            tiles(dve, tile)
            row_max(Tile(0, T - 1))
            attn(Tile(0, T - 1))
            for s in range(STEPS):
                for job in jobs[s]:
                    if job[0] == "fields":
                        weigh(Tile(0, T - 1), job[1])

        @block.tensor
        def _(pe):
            def claim(t, unit, before, behind):
                n = place[unit] - RING
                while n >= 0:
                    old = units[n]
                    there = old and (old[0] == "sample" or (behind if old[0] == "x_t" else before))
                    if there:
                        of = t if old[0] == "sample" else t + 1 if old[0] == "x_t" else t - 1
                        pe.wait_ge(*taken_out(of, old))
                        return
                    n -= RING
                if not t.below(1):
                    assert units[n][0] == "sample"
                    pe.wait_ge(*taken_out(t - 1, units[n]))

            def hidden_of(t, s, before, behind):
                pe.wait_ge(s_native, t.times(STEPS, s + 1))
                for j in range(GROUPS):
                    unit = ("sample", s * GROUPS + j)
                    claim(t, unit, before, behind)
                    if j == NATIVE:
                        pe.wait_ge(s_lo, t.times(STEPS, s + 1))
                    for h in range(2):
                        dst = banks(unit)[:, h, 0:HALF]
                        if j < NATIVE:
                            at = j * PAIRS + h * HALF
                            last = nc.tensor.matmul(dst, attn_wt[:], inner[:, s % 2, at:at + HALF],
                                                    start=True, stop=True)
                            continue
                        at = (j - NATIVE) * PAIRS + h * HALF
                        hi, lo = inner_hi[:, s % 2, at:at + HALF], inner_lo[:, s % 2, at:at + HALF]
                        nc.tensor.matmul(dst, attn_wt_lo[:], hi, start=True, stop=False)
                        nc.tensor.matmul(dst, attn_wt_hi[:], lo, start=False, stop=False)
                        last = nc.tensor.matmul(dst, attn_wt_hi[:], hi, start=False, stop=True)
                    last.then_inc(s_hidden, 1)

            def open_scores(t):
                if not t.below(1):
                    pe.wait_ge(s_exp, t.times(1))
                for h in range(2):
                    nc.tensor.matmul(scores[:, h, 0:HALF], zeros[:, 0:P], zeros[:], start=True, stop=False,
                                     skip_group_check=True)

            def reduce_step(t, s):
                if s == 0:
                    open_scores(t)
                    pe.wait_ge(s_blocks, t.times(1, 1))
                pe.wait_ge(s_fm, t.times(P, (s + 1) * GROUPS))
                for h in range(2):
                    for j in range(GROUPS):
                        at = j * PAIRS + h * HALF
                        last = nc.tensor.matmul(scores[32 * j:32 * j + 32, h, 0:HALF], gnn_blocks[:, j, s, :],
                                                fm[:, s % 2, at:at + HALF], start=False, stop=s == STEPS - 1,
                                                skip_group_check=True)
                last.then_inc(s_red, 1)

            def transpose_x(t, c):
                rows_here(pe, t, [c])
                for n in range(min(FU, F - FU * c)):
                    last = nc.tensor.transpose(banks(("x_t", c))[:, n // FB, n % FB * P:(n % FB + 1) * P],
                                               x_rows[:, FU * c + n, :], ident[:])
                last.then_inc(s_filled["x_t"], 1)

            def work(t, job):
                kind, c = job
                bank = banks(job)
                if kind == "attn_t":
                    if c == 0:
                        pe.wait_ge(s_attn, t.times(1, 1))
                    cols = attn_rows[:].rearrange("p (i c) -> p i c", i=F)
                    for n in range(min(FU, F - FU * c)):
                        last = nc.tensor.transpose(bank[0:2 * FX, n // FB, n % FB * P:(n % FB + 1) * P],
                                                   cols[:, FU * c + n, :], ident[:])
                if kind == "fields":
                    if c == 0:
                        pe.wait_ge(s_emptied["attn_t"], t.times(FUNITS, FUNITS))
                    buf, loads = c % FIELD_BUFS, len(range(c % FIELD_BUFS, YR, FIELD_BUFS))
                    pe.wait_ge(s_fields[buf], t.times(loads * 64, (c // FIELD_BUFS + 1) * 64))
                    for n in range(YS // 2):
                        pair = c * (YS // 2) + n
                        rhs = attn_t[:, :, 2 * pair:2 * pair + 2].rearrange("p i b -> p b i")
                        h, at = divmod(n, YB // 2)
                        last = nc.tensor.matmul(bank[:, h, at * 2 * F:(at + 1) * 2 * F],
                                                x_fields[0:2 * FX, c % FIELD_BUFS, n, :], rhs, start=True, stop=True)
                if kind == "mlp":
                    g = gnn_t[:, bass.ds(t.times(P), P)]
                    w, ins, m_of = ((w1_sb, (g, pooled100[:]), M1),
                                    (w2_sb, [h1[:, k, :] for k in range(K2)], M2),
                                    (w3_sb, [h2[:, k, :] for k in range(M2)], 1))[c]
                    if c == 0:
                        pe.wait_ge(s_pooled100, t.times(1, 1))
                    else:
                        pe.wait_ge(s_emptied[kind], t.times(3, c))
                    for m in range(m_of):
                        for k, z in enumerate(ins):
                            cols = w[:, k, m * P:(m + 1) * P] if c < 2 else w[:, k:k + 1]
                            dst = bank[:, 0, m * P:(m + 1) * P] if c < 2 else bank[0:1, 0, 0:P]
                            last = nc.tensor.matmul(dst, cols, z, start=k == 0, stop=k == len(ins) - 1)
                last.then_inc(s_filled[kind], 1)

            def tile(t, before, behind):
                for s in range(STEPS):
                    hidden_of(t, s, before, behind)
                    if s > 0:
                        reduce_step(t, s - 1)
                    elif before:
                        reduce_step(t - 1, STEPS - 1)
                    for job in jobs[s]:
                        if job[0] == "x_t" and behind:
                            claim(t, job, before, behind)
                            transpose_x(t + 1, job[1])
                        if job[0] != "x_t" and before:
                            claim(t, job, before, behind)
                            work(t - 1, job)

            pe.wait_ge(s_const, 2)
            pe.wait_ge(s_small, 48)
            for i in range(T):
                last = nc.tensor.transpose(ring[0][:, i // 4, i % 4 * P:(i % 4 + 1) * P], gnn_rows[:, i, :], ident[:])
            last.then_inc(s_setup_t, 1)
            nc.tensor.transpose(ring[1][:, 0, 0:P], attn_w_rows, ident[:]).then_inc(s_setup_t, 1)
            pe.wait_ge(s_setup, 6)
            pe.wait_ge(s_weights, 80)
            for c in range(FUNITS):
                if c >= RING:
                    pe.wait_ge(s_emptied["x_t"], c - RING + 1)
                transpose_x(Tile(0, 0), c)
            pe.wait_ge(s_emptied["x_t"], FUNITS)
            pe.wait_ge(s_zero, 4)
            tiles(pe, tile)
            reduce_step(Tile(0, T - 1), STEPS - 1)
            tail = [job for s in range(STEPS) for job in jobs[s] if job[0] != "x_t"]
            for n, job in enumerate(tail):
                same = [old for old in tail[:n] if place[old] % RING == place[job] % RING]
                if same:
                    pe.wait_ge(*taken_out(Tile(0, T - 1), same[-1]))
                else:
                    pe.wait_ge(s_fm, T * P)
                work(Tile(0, T - 1), job)


def kernel(**inputs):
    import numpy as _np
    import concourse.bacc as _bacc
    from concourse import mybir as _mybir
    from concourse.bass_utils import run_bass_kernel_spmd as _run

    nc = _bacc.Bacc("TRN2", target_bir_lowering=False, num_devices=1)
    arrays = {}

    def given(name):
        a = _np.ascontiguousarray(inputs[name])
        arrays[f"in_{name}"] = a
        return nc.dram_tensor(f"in_{name}", a.shape, _mybir.dt.from_np(a.dtype), kind="ExternalInput").ap()

    fields = inputs["ids"].shape[1]
    args = [given("r_gnn_feature"), given("ids"), [given(f"tbl_{f}") for f in range(fields)]]
    args += [given(n) for n in ("W_top1", "b_top1", "W_top2", "b_top2", "W_top3", "L0_rec_attn_W", "L0_rec_attn_b")]
    out = nc.dram_tensor("out_y", (inputs["ids"].shape[0], 1), FP32, kind="ExternalOutput").ap()
    afm_tower(nc, *args, out)
    r = _run(nc, [arrays], core_ids=[0])
    return r.results[0]["out_y"]
```

```python
import concourse.bass as bass
from concourse import mybir
from contextlib import ExitStack

FP32 = mybir.dt.float32
FP32R = mybir.dt.float32r
BF16 = mybir.dt.bfloat16
I32 = mybir.dt.int32
ALU = mybir.AluOpType
ACT = mybir.ActivationFunctionType
AX = mybir.AxisListType


class Tile:

    def __init__(self, loop, ahead):
        self.loop, self.ahead = loop, ahead

    def __add__(self, n):
        return Tile(self.loop, self.ahead + n)

    def __sub__(self, n):
        return Tile(self.loop, self.ahead - n)

    def times(self, each, more=0):
        if isinstance(self.loop, int):
            return (self.loop + self.ahead) * each + more
        return self.loop * each + (self.ahead * each + more)

    def odd(self):
        return (self.loop + self.ahead) % 2

    def below(self, n):
        return isinstance(self.loop, int) and self.loop + self.ahead < n


def afm_tower(nc, gnn, ids, tables, w1, b1, w2, b2, w3, attn_w, attn_b, out):
    P = 128
    B, D = gnn.shape
    F = len(tables)
    T = B // P
    K = (F - 1) // 2
    FX = F + K
    PAIRS = K * F
    HALF = PAIRS // 2
    GROUPS = 4
    STEPS = P // GROUPS
    H1, H2 = w1.shape[1], w2.shape[1]
    M1, M2 = H1 // P, H2 // P
    NATIVES = [2 if s in range(4, 17, 2) else 1 for s in range(STEPS)]
    SPLIT = GROUPS - min(NATIVES)
    FB = 4
    FU = 2 * FB
    FUNITS = -(-F // FU)
    I = F - 1
    QS = P // I
    Q = range(QS)
    YB = 512 // I
    YS = 2 * YB
    YN = YS // QS
    YR = P // YS
    FIELD_BUFS = 2

    FIELDS_AT = (7, 9, 11, 13)
    XT_AT, MLP_AT = (16, 18, 20, 22, 24), (17, 19, 21)
    jobs = {s: [] for s in range(STEPS)}
    for c in range(FUNITS):
        jobs[XT_AT[c]].append(("x_t", c))
    for n in range(YR):
        jobs[FIELDS_AT[n]].append(("fields", n))
    for n in range(3):
        jobs[MLP_AT[n]].append(("mlp", n))
    COUNT = {"fields": YR, "mlp": 3, "x_t": FUNITS}
    SCALE_STEP, TURN_STEP = 2, 3
    REPEAT_STEPS = {XT_AT[c] + 1: c for c in range(K // FU)}
    RING = 3
    units = []
    for s in range(STEPS):
        if s == STEPS - 1:
            units += [None] * (-(len(units) + GROUPS) % RING)
        units += [("sample", s * GROUPS + j) for j in range(GROUPS)] + jobs[s]
    place = {u: n for n, u in enumerate(units) if u}
    left = [job for s in range(STEPS) for job in jobs[s] if job[0] != "x_t"]
    place_alone = {job: n for n, job in enumerate(left)} | {("x_t", c): c for c in range(FUNITS)}

    ctx = ExitStack()
    with ctx:
        def sb(name, shape, dt=FP32):
            return ctx.enter_context(nc.sbuf_tensor(name, shape, dt))

        def pb(name, shape):
            return ctx.enter_context(nc.psum_tensor(name, shape, FP32))

        def sem(name):
            return ctx.enter_context(nc.semaphore(name))

        ids_all = sb("ids_all", [P, T, F], I32)
        ids_now = sb("ids_now", [P, F], I32)
        ids_seen = sb("ids_seen", [P, 1], I32)
        x_rows = sb("x_rows", [P, F, D])
        xt = sb("xt", [D, 2, P, FX])
        inner = sb("inner", [D, 2, GROUPS * PAIRS])
        inner_hi = sb("inner_hi", [D, 2, SPLIT * PAIRS], FP32R)
        inner_lo = sb("inner_lo", [D, 2, SPLIT * PAIRS], FP32R)
        fm = sb("fm", [P, 2, GROUPS * PAIRS])
        gnn_blocks = sb("gnn_blocks", [P, GROUPS, STEPS, STEPS])
        x_fields = sb("x_fields", [P, FIELD_BUFS, YN, D])
        exp_pairs = sb("exp_pairs", [P, F * FX])
        attn = sb("attn", [P, I, I])
        attn_turned = sb("attn_turned", [P, P // QS, I])
        attn_t = sb("attn_t", [P, P, I])
        weighted = sb("weighted", [D, YN, QS, I])
        w1_sb = sb("w1_sb", [P, 2, H1])
        w2_sb = sb("w2_sb", [P, M1, H2])
        w3_sb = sb("w3_sb", [P, M2])
        b1_sb = sb("b1_sb", [P, M1])
        b2_sb = sb("b2_sb", [P, M2])
        attn_wt = sb("attn_wt", [D, P])
        attn_wt_hi = sb("attn_wt_hi", [D, P], FP32R)
        attn_wt_lo = sb("attn_wt_lo", [D, P], FP32R)
        attn_b_sb = sb("attn_b_sb", [P, 1])
        gnn_t = sb("gnn_t", [P, B])
        pooled = sb("pooled", [D, P])
        pooled100 = sb("pooled100", [D, P])
        h1 = sb("h1", [P, M1, P])
        h2 = sb("h2", [P, M2, P])
        y_row = sb("y_row", [1, P])
        ident = sb("ident", [P, P])
        zeros = sb("zeros", [P, HALF], BF16)
        neg_max = sb("neg_max", [P, 1])
        exp_sum = sb("exp_sum", [P, 1])
        inv_sum = sb("inv_sum", [P, 1])
        gnn_rows = x_fields[:, 0, 0:T, :]
        attn_w_rows = x_fields[:, 1, 0, :]

        ring = [pb(f"ring{i}", [P, 2, 512]) for i in range(RING)]
        scores = pb("scores", [P, 2, 512])

        def banks(unit, alone=False):
            return ring[(place_alone if alone else place)[unit] % RING]

        scores_v = scores[:, :, 0:HALF]

        x_dram = nc.dram_tensor("x_dram", (B, F, D), FP32, kind="Internal").ap()

        s_ids = sem("ids_loaded")
        s_ids_now = sem("ids_now_copied")
        s_gather = [sem(f"rows_gathered{c}") for c in range(FUNITS)]
        s_store = sem("rows_stored")
        s_fields = [sem(f"fields_loaded{i}") for i in range(FIELD_BUFS)]
        s_small = sem("small_inputs_loaded")
        s_weights = sem("mlp_weights_loaded")
        s_const = sem("constants_made")
        s_zero = sem("dve_zeros_made")
        s_setup_t = sem("setup_transposed")
        s_setup = sem("setup_copied")
        s_blocks = sem("gnn_blocks_written")
        s_inner = sem("split_inner_ready")
        s_native = sem("native_inner_ready")
        s_hi = sem("inner_hi_ready")
        s_lo = sem("inner_lo_ready")
        s_hidden = sem("hidden_ready")
        s_fm = sem("fm_ready")
        s_red = sem("step_reduced")
        s_max = sem("max_ready")
        s_exp = sem("exp_ready")
        s_inv = sem("softmax_chain")
        s_repeat = sem("fields_repeated")
        s_attn = sem("attn_scaled")
        s_spread = sem("attn_t_quarter_written")
        s_filled = {k: sem(f"{k}_filled") for k in ("fields", "mlp", "x_t")}
        s_emptied = {k: sem(f"{k}_emptied") for k in ("fields", "mlp", "x_t")}
        s_weighted = sem("weighted_ready")
        s_pooled = sem("pooled_summed")
        s_pooled100 = sem("pooled_scaled")
        s_out = sem("out_stored")

        def rows_here(eng, t, units):
            for c in units:
                n = 16 * min(FU, F - FU * c)
                eng.wait_ge(s_gather[c], t.times(n, n))

        def taken_out(t, unit):
            kind, n = unit
            if kind == "sample":
                return s_fm, t.times(P, n + 1)
            if kind == "fields":
                return s_weighted, t.times(YR, n + 1)
            return s_emptied[kind], t.times(COUNT[kind], n + 1)

        block = ctx.enter_context(nc.Block())

        def step(t, s):
            return (t, s) if s < STEPS else (t + 1, s - STEPS)

        def tiles(eng, body):
            body(Tile(0, 0), False, True)
            with eng.Fori(0, T - 2) as loop:
                body(Tile(loop, 1), True, True)
            body(Tile(0, T - 1), True, False)

        @block.sync
        def _(sp):
            sp.dma_start(ids_all[:], ids.rearrange("(t p) f -> p t f", p=P)).then_inc(s_ids, 16)
            sp.dma_start(attn_w_rows, attn_w).then_inc(s_small, 16)
            sp.dma_start(gnn_rows, gnn.rearrange("(t p) a -> p t a", p=P)).then_inc(s_small, 16)
            sp.dma_start(attn_b_sb[:], attn_b.rearrange("(a n) -> a n", n=1), allow_slow_non_contiguous=True).then_inc(s_small, 16)
            sp.dma_start(w1_sb[:], w1[0:2 * P, :].rearrange("(k p) n -> p k n", p=P)).then_inc(s_weights, 16)
            sp.dma_start(h1[:].rearrange("p m b -> p (m b)"), w1[2 * P:3 * P, :]).then_inc(s_weights, 16)
            sp.dma_start(w2_sb[:], w2.rearrange("(k p) n -> p k n", p=P)).then_inc(s_weights, 16)
            sp.dma_start(w3_sb[:], w3.rearrange("(k p) n -> p (k n)", p=P), allow_slow_non_contiguous=True).then_inc(s_weights, 16)
            sp.dma_start(b1_sb[:], b1.rearrange("(m p) -> p m", p=P), allow_slow_non_contiguous=True).then_inc(s_weights, 16)
            sp.dma_start(b2_sb[:], b2.rearrange("(m p) -> p m", p=P), allow_slow_non_contiguous=True).then_inc(s_weights, 16)

            def store_rows(t):
                sp.wait_ge(s_filled["x_t"], t.times(FUNITS, FUNITS))
                sp.dma_start(x_dram[bass.ds(t.times(P), P), :, :], x_rows[:]).then_inc(s_store, 16)

            def load_fields(t, r):
                for q in Q:
                    rows = x_dram[bass.ds(t.times(P, q * I + r * YN), YN), 1:F, :]
                    sp.dma_start(x_fields[q * I:(q + 1) * I, r % FIELD_BUFS], rows.rearrange("n f d -> f n d"))\
                        .then_inc(s_fields[r % FIELD_BUFS], 16)

            def spread_attn(t):
                sp.wait_ge(s_inv, t.times(3, 3))
                for q in Q:
                    own = slice(q * I, (q + 1) * I)
                    sp.dma_start(attn_t[own, own, :], attn_turned[own]).then_inc(s_spread, 16)

            def after(t, store, spread=True):
                for r in range(YR):
                    if r == 0:
                        sp.wait_ge(s_store, t.times(16, 16))
                    if r < FIELD_BUFS and not t.below(1):
                        last = [n for n in range(YR) if n % FIELD_BUFS == r][-1]
                        sp.wait_ge(s_filled["fields"], t.times(YR, last + 1 - YR))
                    if r >= FIELD_BUFS:
                        sp.wait_ge(s_filled["fields"], t.times(YR, r - FIELD_BUFS + 1))
                    load_fields(t, r)
                    if r == FIELD_BUFS - 1 and spread:
                        spread_attn(t)
                if store:
                    store_rows(t + 2)

            store_rows(Tile(0, 0))
            store_rows(Tile(0, 1))
            sp.wait_ge(s_setup, 3)
            after(Tile(0, 0), True)
            with sp.Fori(0, T - 3) as loop:
                after(Tile(loop, 1), True)
            after(Tile(0, T - 2), False)
            after(Tile(0, T - 1), False, False)
            sp.wait_ge(s_store, 16 * T)
            sp.wait_ge(s_out, 16 * T)

        @block.gpsimd
        def _(pool):
            def gather(t, first=False):
                if not first:
                    pool.wait_ge(s_ids_now, t.times(2))
                    rows_here(pool, t - 1, range(FUNITS))
                    pool.wait_ge(s_filled["x_t"], t.times(FUNITS))
                    pool.wait_ge(s_store, t.times(16))
                nc.gpsimd.tensor_copy(ids_now[:], ids_all[:, bass.ds(t.times(1), 1), :].rearrange("p t f -> p (t f)"))\
                    .then_inc(s_ids_now, 1)
                pool.wait_ge(s_ids_now, t.times(2, 1))
                nc.gpsimd.tensor_tensor(ids_seen[:], ids_now[:, 0:1], ids_now[:, 1:2], ALU.add).then_inc(s_ids_now, 1)
                for f in range(F):
                    nc.gpsimd.indirect_dma_start(
                        out=x_rows[:, f, :], out_offset=None, in_=tables[f],
                        in_offset=bass.IndirectOffsetOnAxis(ap=ids_now[:, f:f + 1], axis=0),
                    ).then_inc(s_gather[f // FU], 16)

            nc.gpsimd.memset(ident[:], 1.0).then_inc(s_const, 1)
            pool.wait_ge(s_const, 1)
            nc.gpsimd.affine_select(out=ident[:], in_=ident[:], compare_op=ALU.is_equal, fill=0.0, base=0,
                                    pattern=[[-1, P]], channel_multiplier=1).then_inc(s_const, 1)
            pool.wait_ge(s_const, 2)
            pool.wait_ge(s_ids, 16)
            gather(Tile(0, 0), first=True)
            with pool.Fori(0, T - 1) as loop:
                gather(Tile(loop, 1))

        @block.scalar
        def _(act):
            def relus(t, s, j):
                act.wait_ge(s_hidden, t.times(P, s * GROUPS + j + 1))
                if j == 0 and not (s < 2 and t.below(1)):
                    act.wait_ge(s_red, t.times(STEPS, s - 1))
                dst = fm[:, s % 2, j * PAIRS:(j + 1) * PAIRS].rearrange("p (h n) -> p h n", h=2)
                nc.scalar.activation(dst, banks(("sample", s * GROUPS + j))[:, :, 0:HALF], ACT.Relu,
                                     bias=attn_b_sb[:, 0:1]).then_inc(s_fm, 1)

            def round_inner(t, s):
                act.wait_ge(s_inner, t.times(STEPS, s + 1))
                if not (t.below(1) and s < 2):
                    act.wait_ge(s_hidden, t.times(P, (s - 1) * GROUPS))
                n = (GROUPS - NATIVES[s]) * PAIRS
                nc.scalar.copy(inner_hi[:, s % 2, 0:n], inner[:, s % 2, NATIVES[s] * PAIRS:]).then_inc(s_hi, 1)

            def exps(t):
                act.wait_ge(s_max, t.times(1, 1))
                first = exp_pairs[:, 1:2]
                dst = bass.AP(tensor=first.tensor, offset=first.offset,
                              ap=[first.ap[0], [K // 2, 2], [1, K // 2], [FX + 1, F]])
                nc.scalar.activation(dst, scores_v.rearrange("b h (k i) -> b h k i", i=F), ACT.Exp,
                                     bias=neg_max[:, 0:1], accum_out=exp_sum[:, 0:1]).then_inc(s_exp, 1)

            def scale_attn(t):
                act.wait_ge(s_inv, t.times(3, 1))
                src = exp_pairs[:].rearrange("b (i c) -> b i c", c=FX)[:, 0:I, 1:F]
                nc.scalar.activation(attn[:], src, ACT.Copy, scale=inv_sum[:, 0:1]).then_inc(s_attn, 1)

            def repeat(t, c):
                act.wait_ge(s_emptied["x_t"], t.times(FUNITS, c + 1))
                x = xt[:, bass.ds(t.odd(), 1), :, :].rearrange("d o b f -> d (o b) f")
                nc.scalar.copy(x[:, :, F + FU * c:F + FU * c + FU], x[:, :, FU * c:FU * c + FU]).then_inc(s_repeat, 1)

            def evacuate(t, job, alone=False):
                kind, c = job
                src = banks(job, alone)
                act.wait_ge(s_filled[kind], t.times(COUNT[kind], c + 1))
                if kind == "x_t":
                    n = min(FU, F - FU * c)
                    h = -(-n // FB)
                    src = src[:, 0:h, 0:min(n, FB) * P].rearrange("p h (f b) -> p (h f) b", b=P)
                    dst = xt[:, bass.ds(t.odd(), 1), :, FU * c:FU * c + n].rearrange("d o b f -> d f (o b)")
                    last = nc.scalar.copy(dst, src)
                if kind == "mlp" and c < 2:
                    m, b, h = ((M1, b1_sb, h1), (M2, b2_sb, h2))[c]
                    for i in range(m):
                        last = nc.scalar.activation(h[:, i, :], src[:, 0, i * P:(i + 1) * P],
                                                    ACT.Relu, bias=b[:, i:i + 1])
                if kind == "mlp" and c == 2:
                    if not t.below(1):
                        act.wait_ge(s_out, t.times(16))
                    last = nc.scalar.copy(y_row[:], src[0:1, 0, 0:P])
                last.then_inc(s_emptied[kind], 1)
                if kind == "mlp" and c == 2:
                    act.wait_ge(s_emptied[kind], t.times(3, 3))
                    act.dma_start(out[bass.ds(t.times(P), P), :].rearrange("b n -> n b"), y_row[:]).then_inc(s_out, 16)

            def tile(t, before, behind):
                for s in range(STEPS):
                    relus(t, s, 0)
                    if before and s == 1:
                        exps(t - 1)
                    for j in range(1, GROUPS):
                        relus(t, s, j)
                    if s < STEPS - 2 or behind:
                        round_inner(*step(t, s + 2))
                    if behind and s in REPEAT_STEPS:
                        repeat(t + 1, REPEAT_STEPS[s])
                    if before and s == SCALE_STEP:
                        scale_attn(t - 1)
                    for job in jobs[s]:
                        if job[0] == "x_t" and behind:
                            evacuate(t + 1, job)
                        if job[0] == "mlp" and before:
                            evacuate(t - 1, job)

            act.wait_ge(s_small, 48)
            act.wait_ge(s_weights, 96)
            act.wait_ge(s_setup, 3)
            nc.scalar.copy(attn_wt_hi[:], attn_wt[:]).then_inc(s_setup, 1)
            for c in range(FUNITS):
                evacuate(Tile(0, 0), ("x_t", c), True)
                if c < K // FU:
                    repeat(Tile(0, 0), c)
            for s in range(2):
                round_inner(Tile(0, 0), s)
            tiles(act, tile)
            exps(Tile(0, T - 1))
            scale_attn(Tile(0, T - 1))
            act.wait_ge(s_inv, 3 * T)
            act.wait_ge(s_filled["fields"], (T - 1) * YR)
            for q in Q[:QS // 2]:
                own = slice(q * I, (q + 1) * I)
                nc.scalar.copy(attn_t[own, own, :], attn_turned[own]).then_inc(s_spread, 16)
            for job in left:
                if job[0] == "mlp":
                    evacuate(Tile(0, T - 1), job, True)

        @block.vector
        def _(dve):
            def product(t, s, first, n):
                x = xt[:, bass.ds(t.odd(), 1), first * STEPS + s:(first + n - 1) * STEPS + s + 1:STEPS, :]\
                    .rearrange("d o g f -> d (o g) f")
                lo = x[:, :, 0:F]
                part, sample, field = lo.ap
                lo = bass.AP(tensor=lo.tensor, offset=lo.offset, ap=[part, sample, [0, K], field])
                hi = x[:, :, 1:1 + F]
                hi = bass.AP(tensor=hi.tensor, offset=hi.offset, ap=[part, sample, [1, K], field])
                dst = inner[:, s % 2, first * PAIRS:(first + n) * PAIRS]
                return nc.vector.tensor_tensor(dst.rearrange("d (g k f) -> d g k f", g=n, k=K), lo, hi, ALU.mult)

            def split_product(t, s):
                if not (t.below(1) and s < 2):
                    dve.wait_ge(s_lo, t.times(STEPS, s - 1))
                    if NATIVES[s] < NATIVES[s - 2]:
                        dve.wait_ge(s_hidden, t.times(P, (s - 2) * GROUPS + NATIVES[s - 2]))
                product(t, s, NATIVES[s], GROUPS - NATIVES[s]).then_inc(s_inner, 1)

            def native_product(t, s):
                if not (t.below(1) and s < 2):
                    dve.wait_ge(s_hidden, t.times(P, (s - 2) * GROUPS + min(NATIVES[s], NATIVES[s - 2])))
                product(t, s, 0, NATIVES[s]).then_inc(s_native, 1)

            def rest_of_inner(t, s):
                dve.wait_ge(s_hi, t.times(STEPS, s + 1))
                n = (GROUPS - NATIVES[s]) * PAIRS
                nc.vector.tensor_tensor(inner_lo[:, s % 2, 0:n], inner[:, s % 2, NATIVES[s] * PAIRS:],
                                        inner_hi[:, s % 2, 0:n].bitcast(FP32), ALU.subtract).then_inc(s_lo, 1)

            def gnn_block(t):
                b = gnn_blocks[:].rearrange("a g s c -> a g (s c)")
                dst = b[:, :, 0:(STEPS - 1) * (STEPS + 1) + 1:STEPS + 1]
                src = gnn_t[:, bass.ds(t.times(P), P)].rearrange("a (g s) -> a g s", g=GROUPS)
                nc.vector.tensor_scalar(dst, src, 1.0, None, ALU.mult).then_inc(s_blocks, 1)

            def row_max(t):
                dve.wait_ge(s_red, (t + 1).times(STEPS))
                nc.vector.tensor_reduce(neg_max[:, 0:1], scores_v, AX.XY, ALU.max, negate=True)\
                    .then_inc(s_max, 1)

            def invert_sum(t):
                dve.wait_ge(s_exp, t.times(1, 1))
                nc.vector.reciprocal(inv_sum[:, 0:1], exp_sum[:, 0:1]).then_inc(s_inv, 1)

            def turn_attn(t):
                dve.wait_ge(s_attn, t.times(1, 1))
                pairs = exp_pairs[:].rearrange("b (i c) -> b i c", c=FX)
                far = attn[:, 0:K, K:I]
                nc.vector.scalar_tensor_tensor(far, pairs[:, K + 1:F, F:FX].rearrange("b j i -> b i j"), inv_sum[:, 0:1],
                                               far, ALU.mult, ALU.add).then_inc(s_inv, 1)
                dve.wait_ge(s_inv, t.times(3, 2))
                nc.vector.transpose(attn_turned[:].rearrange("p n i -> p i n"), attn[:])\
                    .then_inc(s_inv, 1)

            def weigh(t, r, alone=False):
                dve.wait_ge(s_filled["fields"], t.times(YR, r + 1))
                own = slice(YN * r, YN * (r + 1))
                x = xt[:, bass.ds(t.odd(), 1), :, 0:I].rearrange("d o (q n) f -> d (o n) q f", q=QS)[:, own]
                y = banks(("fields", r), alone)[:].rearrange("d h c -> d (h c)").rearrange("d (n q f) -> d n q f", q=QS, f=I)
                nc.vector.tensor_tensor(weighted[:], y, x, ALU.mult).then_inc(s_weighted, 1)
                dve.wait_ge(s_weighted, t.times(YR, r + 1))
                nc.vector.tensor_reduce(pooled[:].rearrange("d (q n) -> d n q", q=QS)[:, own], weighted[:], AX.X, ALU.add)\
                    .then_inc(s_pooled, 1)
                dve.wait_ge(s_pooled, t.times(YR, r + 1))
                if r == YR - 1:
                    nc.vector.tensor_scalar(pooled100[:], pooled[:], 100.0, None, ALU.mult)\
                        .then_inc(s_pooled100, 1)

            def tile(t, before, behind):
                for s in range(STEPS):
                    if s == STEPS - 2 and behind:
                        dve.wait_ge(s_emptied["x_t"], (t + 2).times(FUNITS))
                        dve.wait_ge(s_repeat, (t + 2).times(K // FU))
                    if s < STEPS - 2 or behind:
                        split_product(*step(t, s + 2))
                    if s < STEPS - 1 or behind:
                        rest_of_inner(*step(t, s + 1))
                    if s < STEPS - 2 or behind:
                        native_product(*step(t, s + 2))
                    if before and s == 0:
                        row_max(t - 1)
                        gnn_block(t)
                    if before and s == 1:
                        invert_sum(t - 1)
                    if before and s == TURN_STEP:
                        turn_attn(t - 1)
                    for job in jobs[s]:
                        if job[0] == "fields" and before:
                            weigh(t - 1, job[1])

            nc.vector.memset(gnn_blocks[:], 0.0).then_inc(s_zero, 1)
            nc.vector.memset(exp_pairs[:], 0.0).then_inc(s_zero, 1)
            nc.vector.memset(zeros[:], 0.0).then_inc(s_zero, 1)
            nc.vector.memset(attn_t[:], 0.0).then_inc(s_zero, 1)
            dve.wait_ge(s_setup_t, 1)
            nc.vector.tensor_copy(gnn_t[:].rearrange("a (h b) -> a h b", h=2), ring[0][:]).then_inc(s_setup, 1)
            dve.wait_ge(s_setup_t, 2)
            nc.vector.tensor_copy(attn_wt[:], ring[1][:, 0, 0:P]).then_inc(s_setup, 2)
            dve.wait_ge(s_setup, 4)
            nc.vector.tensor_tensor(attn_wt_lo[:], attn_wt[:], attn_wt_hi[:].bitcast(FP32), ALU.subtract)\
                .then_inc(s_setup, 1)
            dve.wait_ge(s_zero, 4)
            dve.wait_ge(s_weights, 96)
            nc.vector.tensor_tensor(w1_sb[:, 0, :], w1_sb[:, 0, :], h1[:].rearrange("p m b -> p (m b)"), ALU.add).then_inc(s_setup, 1)
            gnn_block(Tile(0, 0))
            dve.wait_ge(s_emptied["x_t"], FUNITS)
            dve.wait_ge(s_repeat, K // FU)
            split_product(Tile(0, 0), 0)
            native_product(Tile(0, 0), 0)
            rest_of_inner(Tile(0, 0), 0)
            split_product(Tile(0, 0), 1)
            native_product(Tile(0, 0), 1)
            tiles(dve, tile)
            row_max(Tile(0, T - 1))
            invert_sum(Tile(0, T - 1))
            turn_attn(Tile(0, T - 1))
            dve.wait_ge(s_inv, 3 * T)
            dve.wait_ge(s_filled["fields"], (T - 1) * YR)
            for q in Q[QS // 2:]:
                own = slice(q * I, (q + 1) * I)
                nc.vector.tensor_copy(attn_t[own, own, :], attn_turned[own]).then_inc(s_spread, 16)
            for job in left:
                if job[0] == "fields":
                    weigh(Tile(0, T - 1), job[1], True)

        @block.tensor
        def _(pe):
            def claim(t, unit, before, behind):
                n = place[unit] - RING
                while n >= 0:
                    old = units[n]
                    there = old and (old[0] == "sample" or (behind if old[0] == "x_t" else before))
                    if there:
                        of = t if old[0] == "sample" else t + 1 if old[0] == "x_t" else t - 1
                        pe.wait_ge(*taken_out(of, old))
                        return
                    n -= RING
                if not t.below(1):
                    assert units[n][0] == "sample"
                    pe.wait_ge(*taken_out(t - 1, units[n]))

            def hidden_of(t, s, before, behind):
                native = NATIVES[s]
                pe.wait_ge(s_native, t.times(STEPS, s + 1))
                for j in range(GROUPS):
                    unit = ("sample", s * GROUPS + j)
                    claim(t, unit, before, behind)
                    if j == native:
                        pe.wait_ge(s_lo, t.times(STEPS, s + 1))
                    for h in range(2):
                        dst = banks(unit)[:, h, 0:HALF]
                        if j < native:
                            at = j * PAIRS + h * HALF
                            last = nc.tensor.matmul(dst, attn_wt[:], inner[:, s % 2, at:at + HALF],
                                                    start=True, stop=True)
                            continue
                        at = (j - native) * PAIRS + h * HALF
                        hi, lo = inner_hi[:, s % 2, at:at + HALF], inner_lo[:, s % 2, at:at + HALF]
                        nc.tensor.matmul(dst, attn_wt_lo[:], hi, start=True, stop=False)
                        nc.tensor.matmul(dst, attn_wt_hi[:], lo, start=False, stop=False)
                        last = nc.tensor.matmul(dst, attn_wt_hi[:], hi, start=False, stop=True)
                    last.then_inc(s_hidden, 1)

            def reduce_step(t, s):
                if s == 0:
                    if not t.below(1):
                        pe.wait_ge(s_exp, t.times(1))
                    pe.wait_ge(s_blocks, t.times(1, 1))
                pe.wait_ge(s_fm, t.times(P, (s + 1) * GROUPS))
                for h in range(2):
                    for j in range(GROUPS):
                        at = j * PAIRS + h * HALF
                        last = nc.tensor.matmul(scores[32 * j:32 * j + 32, h, 0:HALF], gnn_blocks[:, j, s, :],
                                                fm[:, s % 2, at:at + HALF], start=s == 0, stop=s == STEPS - 1,
                                                skip_group_check=True)
                last.then_inc(s_red, 1)

            def transpose_x(t, c, alone=False):
                rows_here(pe, t, [c])
                for n in range(min(FU, F - FU * c)):
                    last = nc.tensor.transpose(banks(("x_t", c), alone)[:, n // FB, n % FB * P:(n % FB + 1) * P],
                                               x_rows[:, FU * c + n, :], ident[:])
                last.then_inc(s_filled["x_t"], 1)

            def keep_clock(n):
                for _ in range(n):
                    nc.tensor.matmul(scores[:, 0, 0:HALF], zeros[:, 0:P], zeros[:], start=True, stop=True)

            def work(t, job, alone=False):
                kind, c = job
                bank = banks(job, alone)
                if kind == "fields":
                    if c == 0:
                        pe.wait_ge(s_spread, t.times(16 * QS, 16 * QS))
                    buf, loads = c % FIELD_BUFS, len(range(c % FIELD_BUFS, YR, FIELD_BUFS))
                    pe.wait_ge(s_fields[buf], t.times(loads * 16 * QS, (c // FIELD_BUFS + 1) * 16 * QS))
                    for n in range(YN):
                        rhs = attn_t[:].rearrange("p (q n) i -> p n q i", q=QS)[:, c * YN + n]
                        h, to = divmod(n * QS * I, 512)
                        last = nc.tensor.matmul(bank[:, h, to:to + QS * I], x_fields[:, buf, n, :], rhs,
                                                start=True, stop=True)
                if kind == "mlp":
                    g = gnn_t[:, bass.ds(t.times(P), P)]
                    w, ins, m_of = ((w1_sb, (g, pooled100[:]), M1),
                                    (w2_sb, [h1[:, k, :] for k in range(M1)], M2),
                                    (w3_sb, [h2[:, k, :] for k in range(M2)], 1))[c]
                    if c == 0:
                        pe.wait_ge(s_pooled100, t.times(1, 1))
                    else:
                        pe.wait_ge(s_emptied[kind], t.times(3, c))
                    for m in range(m_of):
                        for k, z in enumerate(ins):
                            cols = w[:, k, m * P:(m + 1) * P] if c < 2 else w[:, k:k + 1]
                            dst = bank[:, 0, m * P:(m + 1) * P] if c < 2 else bank[0:1, 0, 0:P]
                            last = nc.tensor.matmul(dst, cols, z, start=k == 0, stop=k == len(ins) - 1)
                last.then_inc(s_filled[kind], 1)

            def tile(t, before, behind):
                for s in range(STEPS):
                    hidden_of(t, s, before, behind)
                    for job in jobs[s]:
                        if job[0] == "x_t" and behind:
                            claim(t, job, before, behind)
                            transpose_x(t + 1, job[1])
                        if job[0] != "x_t" and before:
                            claim(t, job, before, behind)
                            work(t - 1, job)
                    if s > 0:
                        reduce_step(t, s - 1)
                    elif before:
                        reduce_step(t - 1, STEPS - 1)

            pe.wait_ge(s_const, 2)
            pe.wait_ge(s_small, 48)
            for i in range(T):
                last = nc.tensor.transpose(ring[0][:, i // 4, i % 4 * P:(i % 4 + 1) * P], gnn_rows[:, i, :], ident[:])
            last.then_inc(s_setup_t, 1)
            nc.tensor.transpose(ring[1][:, 0, 0:P], attn_w_rows, ident[:]).then_inc(s_setup_t, 1)
            pe.wait_ge(s_setup, 6)
            pe.wait_ge(s_weights, 96)
            for c in range(FUNITS):
                if c >= RING:
                    pe.wait_ge(s_emptied["x_t"], c - RING + 1)
                transpose_x(Tile(0, 0), c, True)
            pe.wait_ge(s_emptied["x_t"], FUNITS)
            pe.wait_ge(s_zero, 4)
            tiles(pe, tile)
            reduce_step(Tile(0, T - 1), STEPS - 1)
            pe.wait_ge(s_exp, T)
            keep_clock(48)
            for n, job in enumerate(left):
                if n > 0:
                    keep_clock(10)
                if n >= RING:
                    pe.wait_ge(*taken_out(Tile(0, T - 1), left[n - RING]))
                else:
                    pe.wait_ge(s_fm, T * P)
                work(Tile(0, T - 1), job, True)


def kernel(**inputs):
    import numpy as _np
    import concourse.bacc as _bacc
    from concourse import mybir as _mybir
    from concourse.bass_utils import run_bass_kernel_spmd as _run

    nc = _bacc.Bacc("TRN2", target_bir_lowering=False, num_devices=1)
    arrays = {}

    def given(name):
        a = _np.ascontiguousarray(inputs[name])
        arrays[f"in_{name}"] = a
        return nc.dram_tensor(f"in_{name}", a.shape, _mybir.dt.from_np(a.dtype), kind="ExternalInput").ap()

    fields = inputs["ids"].shape[1]
    args = [given("r_gnn_feature"), given("ids"), [given(f"tbl_{f}") for f in range(fields)]]
    args += [given(n) for n in ("W_top1", "b_top1", "W_top2", "b_top2", "W_top3", "L0_rec_attn_W", "L0_rec_attn_b")]
    out = nc.dram_tensor("out_y", (inputs["ids"].shape[0], 1), FP32, kind="ExternalOutput").ap()
    afm_tower(nc, *args, out)
    r = _run(nc, [arrays], core_ids=[0])
    return r.results[0]["out_y"]
```
